# Optimizing a Trainium2 kernel written in Bass

```python
import numpy as np
import jax
import jax.numpy as jnp

def _softmax(x, axis=-1):
    return jax.nn.softmax(x, axis=axis)

def _gelu(x):
    return jax.nn.gelu(x, approximate=True)

def _silu(x):
    return jax.nn.silu(x)

def _sigmoid(x):
    return jax.nn.sigmoid(x)

def _layernorm(x, axis=-1, eps=1e-05):
    m = jnp.mean(x, axis=axis, keepdims=True)
    v = jnp.var(x, axis=axis, keepdims=True)
    return (x - m) / jnp.sqrt(v + eps)

def _scatter_add(tgt, idx, src, axis=0):
    return tgt.at[idx].add(src)

def _segment_sum(src, seg, n):
    return jax.ops.segment_sum(src, seg, n)
kernel_name = 'mk_adj_resnorm_d1_adj_r2_442dab'

def setup_inputs(seed: int=0):
    np.random.seed(seed)
    _w = jnp.asarray

    def _rec_inputs():
        import jax
        import jax.numpy as jnp
        _gk = jax.random.key(seed)
        x = -9.806e-05 + 1 * jax.random.normal(jax.random.fold_in(_gk, 1), (4096, 128), jnp.float32)
        _a = jax.random.bernoulli(jax.random.fold_in(_gk, 2), 0.000976562, (4096, 4096))
        _a = jnp.logical_or(_a, jnp.swapaxes(_a, -1, -2))
        _a = jnp.logical_or(_a, jnp.eye(4096, dtype=bool))
        adj = _a.astype(jnp.int32)
        return (x, adj)
    x, adj = _rec_inputs()

    def _L0_gnn_setup():
        import jax, jax.numpy as jnp
        import numpy as np
        NEG_INF = -9000000000000000.0
        LEAKY_SLOPE = 0.2
        key = jax.random.key(seed)
        k1, k2, k3, k4 = jax.random.split(key, 4)
        N, dim = (2048, 128)
        hidden = jax.random.normal(k1, (N, dim), dtype=jnp.float32)
        adj = jax.random.randint(k2, (N, N), 0, 5)
        W = jax.random.normal(k3, (4, dim), dtype=jnp.float32) * (1.0 / np.sqrt(dim))
        b = jax.random.normal(k4, (4,), dtype=jnp.float32) * 0.01
        return {'hidden': hidden, 'adj': adj, 'W': W, 'b': b}
    _L0_gnn_all = _L0_gnn_setup()
    _L0_gnn_in = {k: v for k, v in _L0_gnn_all.items() if k in ('W', 'b')}
    del _L0_gnn_all
    return {'x': x, 'adj': adj, 'L0_gnn_W': _L0_gnn_in['W'], 'L0_gnn_b': _L0_gnn_in['b']}

def reference(x, adj, L0_gnn_W, L0_gnn_b):
    import jax
    import jax.numpy as jnp

    def _L0_gnn_ref(hidden, adj, W, b):
        import jax, jax.numpy as jnp
        import numpy as np
        NEG_INF = -9000000000000000.0
        LEAKY_SLOPE = 0.2
        hw = hidden[None, :, :] * W[:, None, :]
        e = jnp.einsum('knd,md->knm', hw, hidden) + b[:, None, None]
        e = jax.nn.leaky_relu(e, negative_slope=LEAKY_SLOPE)
        neg = jnp.asarray(NEG_INF, dtype=e.dtype)
        alpha = jnp.where(adj == 1, e[0], neg)
        alpha = jnp.where(adj == 2, e[1], alpha)
        alpha = jnp.where(adj == 3, e[2], alpha)
        alpha = jnp.where(adj == 4, e[3], alpha)
        alpha = jax.nn.softmax(alpha, axis=-1)
        return alpha @ hidden
    x = _layernorm(x + _L0_gnn_ref(x, adj, L0_gnn_W, L0_gnn_b), axis=-1)
    return x

_drawn_inputs = setup_inputs


def setup_inputs(seed=0):
    import zlib

    import numpy as np

    out = dict(_drawn_inputs(seed))
    spreads = {}
    factors = {'L0_gnn_b': 50.318}
    for name, (base, spread) in spreads.items():
        noise = np.random.default_rng([zlib.crc32(name.encode()), seed]).standard_normal(out[name].shape)
        drawn = base * np.exp(spread * noise) if base else spread * noise
        out[name] = jnp.asarray(drawn.astype(out[name].dtype))
    for name, factor in factors.items():
        out[name] = (out[name] * factor).astype(out[name].dtype)
    return out
```

```python
import concourse.bass as bass
from concourse import mybir
from contextlib import ExitStack

P = 128
BANK = 512
SLOPE = 0.2
EPS = 1e-5
NEG = -9000000000000000.0
BIG = 2.0 ** 63
X_SCALE = 16.0
XW_SCALE = 64.0
SCORE_SCALE = X_SCALE * XW_SCALE
PROB_SHIFT = 8.0
FLAG_SCORE = 1e12
FLAG_PART = 32768.0
UNITS = 8


def graph_attention(nc, x_d, adj_d, w_d, b_d, out_d):
    f32, f16, bf16, i32 = mybir.dt.float32, mybir.dt.float16, mybir.dt.bfloat16, mybir.dt.int32
    ALU, ACT, AX = mybir.AluOpType, mybir.ActivationFunctionType, mybir.AxisListType

    N, D = x_d.shape
    HEADS = w_d.shape[0]
    TILES = N // P
    PAIRS = TILES // 2
    HALF = 2 * BANK
    QUARTERS = N // HALF
    BLOCKS = BANK // P
    assert D == P and N == UNITS * BANK and QUARTERS * 2 == UNITS

    x_rows = x_d.rearrange("(t p) d -> p t d", p=P)
    adj_tiles = adj_d.rearrange("(t p) m -> p t m", p=P)
    out_tiles = out_d.rearrange("(t p) d -> p t d", p=P)

    ctx = ExitStack()
    with ctx:
        def sb(name, shape, dt):
            return ctx.enter_context(nc.sbuf_tensor(name, shape, dt))

        def ps(name, shape, dt):
            return ctx.enter_context(nc.psum_tensor(name, shape, dt))

        def sem(name):
            return ctx.enter_context(nc.semaphore(name))

        x16 = sb("x16", [P, TILES, D], f32)
        xparts = sb("xparts", [P, TILES, 2 * D], f16)
        xT_hi = sb("xT_hi", [P, N], f16)
        xT_lo = sb("xT_lo", [P, N], f16)
        xwT_hi = sb("xwT_hi", [P, N], f16)
        xwT_lo = sb("xwT_lo", [P, N], f16)
        adj = sb("adj", [P, 2, N], i32)
        mask = sb("mask", [P, 2, N], bf16)
        relu = sb("relu", [P, 2, HALF], f32)
        probs = sb("probs", [P, 2, N], f32)
        probT_hi = sb("probT_hi", [P, 4, BANK], f16)
        probT_lo = sb("probT_lo", [P, 4, BANK], f16)
        ident = sb("ident", [P, P], f32)
        ident_bf = sb("ident_bf", [P, P], bf16)
        w_col = sb("w_col", [P, HEADS], f32)
        b_all = sb("b_all", [P, HEADS], f32)
        relu_bias = sb("relu_bias", [P, 1], f32)
        chunk_max = sb("chunk_max", [P, 2, QUARTERS], f32)
        row_max = sb("row_max", [P, TILES], f32)
        shift = sb("shift", [P, 2], f32)
        part_sum = sb("part_sum", [P, 2, QUARTERS], f32)
        row_sum = sb("row_sum", [P, 2], f32)
        inv_sum = sb("inv_sum", [P, 2], f32)
        y = sb("y", [P, 2, D], f32)
        stats = sb("stats", [P, 2, 6], f32)
        mean_var = sb("mean_var", [P, 2, 2], f32)
        var_eps = sb("var_eps", [P, 2], f32)
        rstd = sb("rstd", [P, 2], f32)
        minus_half = sb("minus_half", [P, 1], f32)
        normed = sb("normed", [P, 2, D], f32)
        flag_parts = sb("flag_parts", [P, 3], f32)
        flag_scaled = sb("flag_scaled", [P, 3], f32)
        flag_row = sb("flag_row", [P, 1], f32)
        flag_max = sb("flag_max", [P, 1], f32)
        flag_word = sb("flag_word", [P, 1], i32)

        score_ps = ps("score_ps", [P, 2, HALF], f32)
        trans_ps = ps("trans_ps", [P, 2, BANK], f32)
        mixed_ps = ps("mixed_ps", [P, 2, BANK], f32)

        x_loaded = [sem(f"x_loaded{c}") for c in range(QUARTERS)]
        small_loaded = sem("small_loaded")
        cleared = sem("cleared")
        ident_ready = sem("ident_ready")
        x_scaled = sem("x_scaled")
        xparts_hi = sem("xparts_hi")
        xparts_ready = sem("xparts_ready")
        xT_ready = sem("xT_ready")
        xT_hi_ready = sem("xT_hi_ready")
        xw_ready = sem("xw_ready")
        xw_hi_ready = sem("xw_hi_ready")
        xT_split = sem("xT_split")
        bias_ready = sem("bias_ready")
        passed = sem("passed")
        adj_loaded = [sem(f"adj_loaded{s}") for s in range(2)]
        mask_ready = sem("mask_ready")
        scores_ready = sem("scores_ready")
        relu_ready = sem("relu_ready")
        leaky_ready = sem("leaky_ready")
        max_ready = sem("max_ready")
        shift_ready = sem("shift_ready")
        probs_ready = sem("probs_ready")
        transposed = sem("transposed")
        high_ready = sem("high_ready")
        low_ready = sem("low_ready")
        mixed = sem("mixed")
        sum_ready = sem("sum_ready")
        inv_ready = sem("inv_ready")
        y_ready = sem("y_ready")
        stats_ready = sem("stats_ready")
        var_ready = sem("var_ready")
        eps_added = sem("eps_added")
        rstd_ready = sem("rstd_ready")
        norm_ready = sem("norm_ready")
        stored = [sem(f"stored{s}") for s in range(2)]
        flag_step = sem("flag_step")
        flag_local = sem("flag_local")
        flag_step_pool = sem("flag_step_pool")
        flag_ready = sem("flag_ready")
        g_transposed = sem("g_transposed")
        g_xT = sem("g_xT")
        g_adj = sem("g_adj")
        g_xw = sem("g_xw")
        g_scores = sem("g_scores")
        g_dve = sem("g_dve")
        g_alpha = sem("g_alpha")
        g_read = sem("g_read")
        g_probs = sem("g_probs")
        g_probT = sem("g_probT")
        g_copied = sem("g_copied")
        g_mixed = sem("g_mixed")
        g_var = sem("g_var")
        g_pool = sem("g_pool")
        g_norm = sem("g_norm")
        g_stored = sem("g_stored")

        block = ctx.enter_context(nc.Block())

        def back(r, lag):
            return (r - lag) // UNITS, (r - lag) % UNITS

        def exists(tile):
            return not isinstance(tile, int) or 0 <= tile < TILES

        def first(tile, n=1):
            return isinstance(tile, int) and tile < n

        def over_pairs(eng, pair, peeled, drained=2):
            for j in range(peeled):
                pair(j)
            with eng.Fori(peeled, PAIRS) as j:
                pair(j)
            for j in range(PAIRS, PAIRS + drained):
                pair(j)

        def settled(eng):
            eng.sem_inc(passed, 1)

        T_LAG = 12
        HI_LAG = T_LAG
        LO_LAG = T_LAG + 1
        MIX_LAG = T_LAG + 2
        EXP_LAG = 10
        TAIL_LAG = MIX_LAG + 2 + UNITS - 1

        @block.sync
        def _(sp):
            for c in range(QUARTERS):
                n = TILES // QUARTERS
                sp.dma_start(x16[:, n * c:n * c + n, :], x_rows[:, n * c:n * c + n, :]).then_inc(x_loaded[c], 16)
                if c == 0:
                    sp.dma_start(adj[:, 0, :], adj_tiles[:, 0, :]).then_inc(adj_loaded[0], 16)
            sp.dma_start(adj[:, 1, :], adj_tiles[:, 1, :]).then_inc(adj_loaded[1], 16)

            STORE_LAG = 5

            def pair(j):
                for s in range(2):
                    i = 2 * j + s
                    if exists(i) and not first(i, 2):
                        sp.wait_ge(mask_ready, i - 1)
                        sp.dma_start(adj[:, s, :], adj_tiles[:, bass.ds(i, 1), :]).then_inc(adj_loaded[s], 16)
                    k = i - STORE_LAG
                    if exists(k):
                        store(k, 1 - s)

            def store(k, s):
                sp.wait_ge(norm_ready, k + 1)
                sp.dma_start(out_tiles[:, bass.ds(k, 1), :], normed[:, s, :]).then_inc(stored[s], 16)

            over_pairs(sp, pair, peeled=3, drained=3)
            for s in range(2):
                sp.wait_ge(stored[s], 16 * PAIRS)

            sp.wait_ge(flag_ready, 1)
            general = sp.value_load(flag_word[0:1, 0:1], min_val=0, max_val=1)
            with sp.If(general > 0):
                with sp.Fori(0, TILES) as t:
                    sp.dma_start(adj[:, 0, :], adj_tiles[:, bass.ds(t, 1), :]).then_inc(g_adj, 16)
                    sp.wait_ge(g_norm, t + 1)
                    sp.dma_start(out_tiles[:, bass.ds(t, 1), :], normed[:, 0, :]).then_inc(g_stored, 16)
                sp.wait_ge(g_stored, 16 * TILES)
            sp.nop()

        @block.gpsimd
        def _(pool):
            nc.gpsimd.memset(ident[:, :], 0.0).then_inc(cleared, 1)
            nc.gpsimd.memset(ident_bf[:, :], 0.0).then_inc(cleared, 1)
            nc.gpsimd.memset(minus_half[:, :], -0.5).then_inc(cleared, 1)
            pool.wait_ge(cleared, 3)
            for m in (ident, ident_bf):
                nc.gpsimd.affine_select(out=m[:, :], in_=m[:, :], compare_op=ALU.not_equal, fill=1.0, base=0,
                                        pattern=[[-1, P]], channel_multiplier=1).then_inc(ident_ready, 1)

            def make_mask(i, s):
                pool.wait_ge(adj_loaded[s], 8 * (i - s) + 16)
                if not first(i, 2):
                    pool.wait_ge(scores_ready, UNITS * i - UNITS)
                settled(pool)
                nc.gpsimd.tensor_scalar(mask[:, s, :], adj[:, s, :], -1.0, BIG,
                                        ALU.add, ALU.mult).then_inc(mask_ready, 1)

            n = TILES // QUARTERS
            for c in range(QUARTERS):
                rows = slice(n * c, n * c + n)
                pool.wait_ge(x_loaded[c], 16)
                nc.gpsimd.tensor_scalar(x16[:, rows, :], x16[:, rows, :], X_SCALE, None,
                                        ALU.mult).then_inc(x_scaled, 1)
                if c == 0:
                    make_mask(0, 0)
            make_mask(1, 1)
            for c in range(QUARTERS):
                rows = slice(n * c, n * c + n)
                pool.wait_ge(x_scaled, c + 1)
                nc.gpsimd.tensor_copy(xparts[:, rows, 0:D], x16[:, rows, :]).then_inc(xparts_hi, 1)
                pool.wait_ge(xparts_hi, c + 1)
                nc.gpsimd.tensor_tensor(xparts[:, rows, D:2 * D], x16[:, rows, :], xparts[:, rows, 0:D],
                                        ALU.subtract).then_inc(xparts_ready, 1)

            def layer_norm(i, s):
                pool.wait_ge(var_ready, i + 1)
                settled(pool)
                nc.gpsimd.tensor_scalar(var_eps[:, s:s + 1], mean_var[:, s, 1:2], EPS * X_SCALE * X_SCALE, None,
                                        ALU.add).then_inc(eps_added, 1)
                pool.wait_ge(eps_added, i + 1)
                nc.gpsimd.tensor_tensor(rstd[:, s:s + 1], var_eps[:, s:s + 1], minus_half[:, :],
                                        ALU.pow).then_inc(rstd_ready, 1)
                pool.wait_ge(rstd_ready, i + 1)
                if not first(i, 2):
                    pool.wait_ge(stored[s], 8 * (i - s))
                settled(pool)
                nc.gpsimd.tensor_scalar(normed[:, s, :], y[:, s, :], mean_var[:, s, 0:1], rstd[:, s:s + 1],
                                        ALU.subtract, ALU.mult).then_inc(norm_ready, 1)

            def pair(j):
                for s in range(2):
                    i = 2 * j + s
                    if exists(i) and not first(i, 2):
                        make_mask(i, s)
                    if exists(i - 3):
                        layer_norm(i - 3, 1 - s)

            over_pairs(pool, pair, peeled=3, drained=1)

            pool.wait_ge(flag_local, 1)
            nc.gpsimd.partition_all_reduce(flag_max[:, :], flag_row[:, :], P,
                                           bass.bass_isa.ReduceOp.max).then_inc(flag_step_pool, 1)
            pool.wait_ge(flag_step_pool, 1)
            nc.gpsimd.tensor_scalar(flag_word[:, :], flag_max[:, :], 1.0, None, ALU.is_gt).then_inc(flag_ready, 1)
            layer_norm(TILES - 1, 1)
            pool.wait_ge(flag_ready, 1)
            general = pool.value_load(flag_word[0:1, 0:1], min_val=0, max_val=1)
            with pool.If(general > 0):
                for s in range(2):
                    pool.wait_ge(stored[s], 16 * PAIRS)
                with pool.Fori(0, TILES) as t:
                    pool.wait_ge(g_var, t + 1)
                    settled(pool)
                    nc.gpsimd.tensor_scalar(var_eps[:, 0:1], mean_var[:, 0, 1:2], EPS * X_SCALE * X_SCALE, None,
                                            ALU.add).then_inc(g_pool, 1)
                    pool.wait_ge(g_pool, 2 * t + 1)
                    nc.gpsimd.tensor_tensor(rstd[:, 0:1], var_eps[:, 0:1], minus_half[:, :],
                                            ALU.pow).then_inc(g_pool, 1)
                    pool.wait_ge(g_pool, 2 * t + 2)
                    settled(pool)
                    nc.gpsimd.tensor_scalar(normed[:, 0, :], y[:, 0, :], mean_var[:, 0, 0:1], rstd[:, 0:1],
                                            ALU.subtract, ALU.mult).then_inc(g_norm, 1)
                    pool.wait_ge(g_stored, 16 * t + 16)
            pool.nop()

        @block.tensor
        def _(pe):
            pe.wait_ge(ident_ready, 2)
            for c in range(QUARTERS):
                pe.wait_ge(x_scaled, c + 1)
                if c >= 2:
                    pe.wait_ge(xT_split, c - 1)
                for k in range(HALF // P):
                    last = nc.tensor.transpose(score_ps[:, c % 2, P * k:P * k + P],
                                               x16[:, HALF // P * c + k, :], ident[:, :])
                last.then_inc(xT_ready, 1)

            def scores(j, r):
                off, u = back(r, 0)
                i = 2 * j + off
                if not exists(i):
                    return
                c, h = u // 2, u % 2
                if isinstance(j, int) and j == 0 and off == 0:
                    pe.wait_ge(xT_split, QUARTERS)
                if u == 0:
                    pe.wait_ge(mask_ready, i + 1)
                if h == 0 and not (isinstance(i, int) and QUARTERS * i + c < 2):
                    pe.wait_ge(leaky_ready, QUARTERS * i + c - 1)
                out = score_ps[:, c % 2, h * BANK:h * BANK + BANK]
                cols = slice(u * BANK, u * BANK + BANK)
                rows = bass.ds(P * i, P)
                nc.tensor.matmul(out, ident_bf[:, :], mask[:, off, cols], start=True, stop=False)
                nc.tensor.matmul(out, xwT_hi[:, rows], xT_hi[:, cols], start=False, stop=False)
                nc.tensor.matmul(out, xwT_hi[:, rows], xT_lo[:, cols], start=False, stop=False)
                nc.tensor.matmul(out, xwT_lo[:, rows], xT_hi[:, cols], start=False, stop=True)\
                    .then_inc(scores_ready, 1)

            def transposes(j, r):
                off, g = back(r, T_LAG)
                i = 2 * j + off
                if not exists(i):
                    return
                if g % 2 == 0:
                    pe.wait_ge(probs_ready, QUARTERS * i + g // 2 + 1)
                if not (isinstance(i, int) and UNITS * i + g < 2):
                    pe.wait_ge(low_ready, UNITS * i + g - 1)
                for k in range(BLOCKS):
                    m = g * BANK + k * P
                    last = nc.tensor.transpose(trans_ps[:, g % 2, P * k:P * k + P], probs[:, off % 2, m:m + P],
                                               ident[:, :])
                last.then_inc(transposed, 1)

            def mix(j, r):
                off, g = back(r, MIX_LAG)
                i = 2 * j + off
                if not exists(i):
                    return
                out = mixed_ps[:, off % 2, 0:D]
                pe.wait_ge(low_ready, UNITS * i + g + 1)
                if g == 0:
                    if not first(i, 2):
                        pe.wait_ge(y_ready, i - 1)
                    if first(i):
                        pe.wait_ge(xparts_ready, QUARTERS)
                for k in range(BLOCKS):
                    m = g * BLOCKS + k
                    hi = probT_hi[:, g % 4, P * k:P * k + P]
                    lo = probT_lo[:, g % 4, P * k:P * k + P]
                    nc.tensor.matmul(out, hi, xparts[:, m, 0:D], start=(m == 0), stop=False)
                    nc.tensor.matmul(out, hi, xparts[:, m, D:2 * D], start=False, stop=False)
                    last = nc.tensor.matmul(out, lo, xparts[:, m, 0:D], start=False, stop=(m == TILES - 1))
                last.then_inc(mixed, 1)

            def pair(j):
                for r in range(2 * UNITS):
                    scores(j, r)
                    transposes(j, r)
                    mix(j, r)

            over_pairs(pe, pair, peeled=2)

            pe.wait_ge(flag_ready, 1)
            general = pe.value_load(flag_word[0:1, 0:1], min_val=0, max_val=1)
            with pe.If(general > 0):
                for c in range(QUARTERS):
                    if c >= 2:
                        pe.wait_ge(g_xT, c - 1)
                    for k in range(HALF // P):
                        last = nc.tensor.transpose(score_ps[:, c % 2, P * k:P * k + P],
                                                   x16[:, HALF // P * c + k, :], ident[:, :])
                    last.then_inc(g_transposed, 1)
                pe.wait_ge(g_xT, QUARTERS)
                with pe.Fori(0, TILES) as t:
                    pe.wait_ge(g_xw, t + 1)
                    for n in range(HEADS * UNITS):
                        u, k = n // HEADS, n % HEADS
                        if n >= 2:
                            pe.wait_ge(g_read, HEADS * UNITS * t + n - 1)
                        nc.tensor.matmul(score_ps[:, n % 2, 0:BANK], relu[:, 0, P * k:P * k + P],
                                         probs[:, 1, u * BANK:u * BANK + BANK], start=True, stop=True)\
                            .then_inc(g_scores, 1)
                    pe.wait_ge(g_probs, t + 1)
                    for g in range(UNITS):
                        for k in range(BLOCKS):
                            m = g * BANK + k * P
                            last = nc.tensor.transpose(trans_ps[:, 0, P * k:P * k + P], probs[:, 0, m:m + P],
                                                       ident[:, :])
                        last.then_inc(g_probT, 1)
                        pe.wait_ge(g_copied, UNITS * t + g + 1)
                        for k in range(BLOCKS):
                            m = g * BLOCKS + k
                            last = nc.tensor.matmul(mixed_ps[:, 0, 0:D], relu[:, 1, P * k:P * k + P],
                                                    x16[:, m, :], start=(m == 0), stop=(m == TILES - 1))
                        last.then_inc(g_mixed, 1)
            pe.nop()

        @block.scalar
        def _(act):
            act.dma_start(w_col[:, :], w_d.rearrange("k d -> d k"), allow_slow_non_contiguous=True).then_inc(small_loaded, 16)
            act.dma_start(b_all[:, :], b_d.rearrange("(a k) -> a k", a=1).broadcast_to([P, HEADS]))\
                .then_inc(small_loaded, 16)
            for c in range(QUARTERS):
                cols = slice(HALF * c, HALF * c + HALF)
                act.wait_ge(xT_ready, c + 1)
                nc.scalar.activation(xT_hi[:, cols], score_ps[:, c % 2, :], ACT.Copy).then_inc(xT_hi_ready, 1)
                act.wait_ge(xw_ready, c + 1)
                nc.scalar.activation(xwT_hi[:, cols], relu[:, c % 2, :], ACT.Copy).then_inc(xw_hi_ready, 1)
            act.wait_ge(bias_ready, 1)

            def do_relu(j, r):
                off, u = back(r, 1)
                i = 2 * j + off
                if u % 2 or not exists(i):
                    return
                q = QUARTERS * i + u // 2
                s = (u // 2) % 2
                act.wait_ge(scores_ready, UNITS * i + u + 2)
                if isinstance(q, int) and q < 2:
                    act.wait_ge(xT_split, QUARTERS)
                else:
                    act.wait_ge(leaky_ready, q - 1)
                nc.scalar.activation(relu[:, s, :], score_ps[:, s, :], ACT.Relu, bias=relu_bias[:, :],
                                     scale=1.0 / SLOPE - 1.0).then_inc(relu_ready, 1)

            def do_exp(j, r):
                off, u = back(r, EXP_LAG)
                i = 2 * j + off
                if u % 2 or not exists(i):
                    return
                s, c = off % 2, u // 2
                if c == 0:
                    act.wait_ge(shift_ready, i + 1)
                    if not first(i, 2):
                        act.wait_ge(sum_ready, i - 1)
                part = probs[:, s, HALF * c:HALF * c + HALF]
                nc.scalar.activation(part, part, ACT.Exp, bias=shift[:, s:s + 1],
                                     accum_out=part_sum[:, s, c:c + 1]).then_inc(probs_ready, 1)

            def do_high(j, r):
                off, g = back(r, HI_LAG)
                i = 2 * j + off
                if not exists(i):
                    return
                act.wait_ge(transposed, UNITS * i + g + 1)
                if not (isinstance(i, int) and UNITS * i + g < 4):
                    act.wait_ge(mixed, UNITS * i + g - 3)
                nc.scalar.activation(probT_hi[:, g % 4, :], trans_ps[:, g % 2, :], ACT.Copy).then_inc(high_ready, 1)

            def pair(j):
                for r in range(2 * UNITS):
                    do_relu(j, r)
                    do_exp(j, r)
                    do_high(j, r)

            over_pairs(act, pair, peeled=2)

            act.wait_ge(flag_ready, 1)
            general = act.value_load(flag_word[0:1, 0:1], min_val=0, max_val=1)
            with act.If(general > 0):
                for c in range(QUARTERS):
                    act.wait_ge(g_transposed, c + 1)
                    nc.scalar.activation(probs[:, 1, HALF * c:HALF * c + HALF], score_ps[:, c % 2, :],
                                         ACT.Copy).then_inc(g_xT, 1)
                with act.Fori(0, TILES) as t:
                    act.wait_ge(g_alpha, t + 1)
                    nc.scalar.activation(probs[:, 0, :], probs[:, 0, :], ACT.Exp, bias=shift[:, 0:1],
                                         accum_out=part_sum[:, 0, 0:1]).then_inc(g_probs, 1)
                    for g in range(UNITS):
                        act.wait_ge(g_probT, UNITS * t + g + 1)
                        if g:
                            act.wait_ge(g_mixed, UNITS * t + g)
                        nc.scalar.activation(relu[:, 1, 0:BANK], trans_ps[:, 0, :], ACT.Copy).then_inc(g_copied, 1)
            act.nop()

        @block.vector
        def _(dve):
            dve.wait_ge(small_loaded, 32)
            nc.vector.tensor_scalar(relu_bias[:, :], b_all[:, 0:1], (1.0 / SLOPE - 1.0) * SCORE_SCALE, None,
                                    ALU.mult).then_inc(bias_ready, 1)
            for c in range(QUARTERS):
                cols = slice(HALF * c, HALF * c + HALF)
                dve.wait_ge(xT_ready, c + 1)
                dve.wait_ge(xT_hi_ready, c + 1)
                if c >= 2:
                    dve.wait_ge(xw_hi_ready, c - 1)
                nc.vector.tensor_scalar(relu[:, c % 2, :], score_ps[:, c % 2, :], w_col[:, 0:1],
                                        XW_SCALE / X_SCALE, ALU.mult, ALU.mult).then_inc(xw_ready, 1)
                nc.vector.tensor_tensor(xT_lo[:, cols], score_ps[:, c % 2, :], xT_hi[:, cols], ALU.subtract)
                dve.wait_ge(xw_hi_ready, c + 1)
                dve.wait_ge(xw_ready, c + 1)
                nc.vector.tensor_tensor(xwT_lo[:, cols], relu[:, c % 2, :], xwT_hi[:, cols],
                                        ALU.subtract).then_inc(xT_split, 1)

            def do_low(j, r):
                off, g = back(r, LO_LAG)
                i = 2 * j + off
                if not exists(i):
                    return
                dve.wait_ge(high_ready, UNITS * i + g + 1)
                if not (isinstance(i, int) and UNITS * i + g < 4):
                    dve.wait_ge(mixed, UNITS * i + g - 3)
                nc.vector.tensor_tensor(probT_lo[:, g % 4, :], trans_ps[:, g % 2, :], probT_hi[:, g % 4, :],
                                        ALU.subtract).then_inc(low_ready, 1)

            def do_leaky(j, r):
                off, u = back(r, 2)
                i = 2 * j + off
                if u % 2 or not exists(i):
                    return
                c, s = u // 2, off % 2
                q = QUARTERS * i + c
                dve.wait_ge(relu_ready, q + 1)
                if not first(i, 2):
                    dve.wait_ge(transposed, UNITS * i - 2 * UNITS + 2 * c + 2)
                settled(dve)
                nc.vector.tensor_tensor_reduce(
                    out=probs[:, s, HALF * c:HALF * c + HALF], in0=score_ps[:, c % 2, :], in1=relu[:, c % 2, :],
                    scale=SLOPE / SCORE_SCALE, scalar=-3e38, op0=ALU.add, op1=ALU.max,
                    accum_out=chunk_max[:, s, c:c + 1]).then_inc(leaky_ready, 1)
                if c == QUARTERS - 1:
                    dve.wait_ge(leaky_ready, QUARTERS * i + QUARTERS)
                    nc.vector.tensor_reduce(row_max[:, bass.ds(i, 1)], chunk_max[:, s, :], AX.X, ALU.max)\
                        .then_inc(max_ready, 1)
                    dve.wait_ge(max_ready, i + 1)
                    nc.vector.tensor_scalar(shift[:, s:s + 1], row_max[:, bass.ds(i, 1)], -1.0, PROB_SHIFT,
                                            ALU.mult, ALU.add).then_inc(shift_ready, 1)

            def do_tail(j, r):
                off, u = back(r, TAIL_LAG)
                i = 2 * j + off
                if u or not exists(i):
                    return
                s = off % 2
                dve.wait_ge(probs_ready, QUARTERS * i + QUARTERS)
                nc.vector.tensor_reduce(row_sum[:, s:s + 1], part_sum[:, s, :], AX.X, ALU.add).then_inc(sum_ready, 1)
                dve.wait_ge(sum_ready, i + 1)
                nc.vector.reciprocal(inv_sum[:, s:s + 1], row_sum[:, s:s + 1]).then_inc(inv_ready, 1)
                dve.wait_ge(inv_ready, i + 1)
                dve.wait_ge(mixed, UNITS * i + UNITS)
                if not first(i, 2):
                    dve.wait_ge(norm_ready, i - 1)
                nc.vector.scalar_tensor_tensor(out=y[:, s, :], in0=mixed_ps[:, s, 0:D], scalar=inv_sum[:, s:s + 1],
                                               in1=x16[:, bass.ds(i, 1), :].rearrange("p a d -> p (a d)"),
                                               op0=ALU.mult, op1=ALU.add).then_inc(y_ready, 1)
                dve.wait_ge(y_ready, i + 1)
                nc.vector.bn_stats(stats[:, s, :], y[:, s, :]).then_inc(stats_ready, 1)
                dve.wait_ge(stats_ready, i + 1)
                settled(dve)
                nc.vector.bn_aggr(mean_var[:, s, :], stats[:, s, :]).then_inc(var_ready, 1)

            def do_flags():
                for n, (part, unit) in enumerate(((row_max, FLAG_SCORE), (xT_hi, FLAG_PART), (xwT_hi, FLAG_PART))):
                    nc.vector.tensor_reduce(flag_parts[:, n:n + 1], part[:, :], AX.X, ALU.max,
                                            apply_absolute_value=True).then_inc(flag_step, 1)
                    dve.wait_ge(flag_step, 2 * n + 1)
                    nc.vector.tensor_scalar(flag_scaled[:, n:n + 1], flag_parts[:, n:n + 1], 1.0 / unit, None,
                                            ALU.mult).then_inc(flag_step, 1)
                dve.wait_ge(flag_step, 6)
                nc.vector.tensor_reduce(flag_row[:, :], flag_scaled[:, :], AX.X, ALU.max).then_inc(flag_local, 1)

            def pair(j):
                for r in range(2 * UNITS):
                    do_low(j, r)
                    do_leaky(j, r)
                    if isinstance(j, int) and j == PAIRS and r == 3:
                        do_flags()
                    do_tail(j, r)

            over_pairs(dve, pair, peeled=2)

            dve.wait_ge(flag_ready, 1)
            general = dve.value_load(flag_word[0:1, 0:1], min_val=0, max_val=1)
            with dve.If(general > 0):
                dve.wait_ge(norm_ready, TILES)
                dve.wait_ge(mask_ready, TILES)
                STEPS = HEADS + UNITS * (3 + 3 * HEADS) + 4
                with dve.Fori(0, TILES) as t:
                    done = 0

                    def own(instruction):
                        nonlocal done
                        done += 1
                        instruction.then_inc(g_dve, 1)
                        dve.wait_ge(g_dve, STEPS * t + done)

                    dve.wait_ge(g_xT, QUARTERS)
                    dve.wait_ge(g_adj, 16 * t + 16)
                    for k in range(HEADS):
                        own(nc.vector.tensor_scalar(relu[:, 0, P * k:P * k + P],
                                                    probs[:, 1, bass.ds(P * t, P)],
                                                    w_col[:, k:k + 1], None, ALU.mult))
                    nc.vector.tensor_copy(row_sum[:, 1:2], row_sum[:, 0:1]).then_inc(g_xw, 1)
                    for u in range(UNITS):
                        cols = slice(u * BANK, u * BANK + BANK)
                        alpha, a = probs[:, 0, cols], adj[:, 0, cols]
                        tmp = [adj[:, 1, n * BANK:n * BANK + BANK].bitcast(f32) for n in range(3)]
                        own(nc.vector.tensor_scalar(tmp[0], a, 1.0, NEG, ALU.is_lt, ALU.mult))
                        own(nc.vector.tensor_scalar(tmp[1], a, float(HEADS), NEG, ALU.is_gt, ALU.mult))
                        own(nc.vector.tensor_tensor(alpha, tmp[0], tmp[1], ALU.add))
                        for k in range(HEADS):
                            n = HEADS * u + k
                            dve.wait_ge(g_scores, HEADS * UNITS * t + n + 1)
                            nc.vector.tensor_scalar(tmp[0], score_ps[:, n % 2, 0:BANK], 1.0 / X_SCALE / X_SCALE,
                                                    b_all[:, k:k + 1], ALU.mult, ALU.add).then_inc(g_read, 1)
                            dve.wait_ge(g_read, HEADS * UNITS * t + n + 1)
                            own(nc.vector.scalar_tensor_tensor(out=tmp[1], in0=tmp[0], scalar=SLOPE, in1=tmp[0],
                                                               op0=ALU.mult, op1=ALU.max))
                            own(nc.vector.scalar_tensor_tensor(out=tmp[2], in0=a, scalar=float(k + 1), in1=tmp[1],
                                                               op0=ALU.is_equal, op1=ALU.mult))
                            own(nc.vector.tensor_tensor(alpha, alpha, tmp[2], ALU.add))
                    own(nc.vector.tensor_reduce(chunk_max[:, 0, 0:1], probs[:, 0, :], AX.X, ALU.max))
                    nc.vector.tensor_scalar(shift[:, 0:1], chunk_max[:, 0, 0:1], -1.0, None,
                                            ALU.mult).then_inc(g_alpha, 1)
                    dve.wait_ge(g_probs, t + 1)
                    own(nc.vector.reciprocal(inv_sum[:, 0:1], part_sum[:, 0, 0:1]))
                    dve.wait_ge(g_mixed, UNITS * t + UNITS)
                    own(nc.vector.scalar_tensor_tensor(out=y[:, 0, :], in0=mixed_ps[:, 0, 0:D],
                                                       scalar=inv_sum[:, 0:1],
                                                       in1=x16[:, bass.ds(t, 1), :].rearrange("p a d -> p (a d)"),
                                                       op0=ALU.mult, op1=ALU.add))
                    own(nc.vector.bn_stats(stats[:, 0, :], y[:, 0, :]))
                    settled(dve)
                    nc.vector.bn_aggr(mean_var[:, 0, :], stats[:, 0, :]).then_inc(g_var, 1)
                    dve.wait_ge(g_norm, t + 1)
                    STEPS_USED = done
                assert STEPS_USED == HEADS + UNITS * (3 + 3 * HEADS) + 4, STEPS_USED
            dve.nop()


_INS = ["x", "adj", "L0_gnn_W", "L0_gnn_b"]


def kernel(**inputs):
    import numpy as np
    import concourse.bacc as bacc
    from concourse import mybir as mb
    from concourse.bass_utils import run_bass_kernel_spmd

    nc = bacc.Bacc("TRN2", target_bir_lowering=False, num_devices=1)
    arrays, args = {}, []
    for name in _INS:
        a = np.ascontiguousarray(inputs[name])
        arrays[f"in_{name}"] = a
        args.append(nc.dram_tensor(f"in_{name}", a.shape, mb.dt.from_np(a.dtype), kind="ExternalInput").ap())
    out = nc.dram_tensor("out", inputs["x"].shape, mb.dt.float32, kind="ExternalOutput").ap()
    graph_attention(nc, *args, out)
    return run_bass_kernel_spmd(nc, [arrays], core_ids=[0]).results[0]["out"]
```

```python
import concourse.bass as bass
from concourse import mybir
from contextlib import ExitStack

P = 128
BANK = 512
SLOPE = 0.2
EPS = 1e-5
NEG = -9000000000000000.0
BIG = 2.0 ** 63
X_SCALE = 16.0
XW_SCALE = 64.0
PROB_SCALE = 4096.0
SCORE_SCALE = X_SCALE * XW_SCALE
PAD = 2.0 ** -20
TINY_SUM = 1e-30
FLAG_SCORE = 1e15
FLAG_PART = 32768.0
UNITS = 8


def graph_attention(nc, x_d, adj_d, w_d, b_d, out_d):
    f32, f16, bf16, i32 = mybir.dt.float32, mybir.dt.float16, mybir.dt.bfloat16, mybir.dt.int32
    ALU, ACT, AX = mybir.AluOpType, mybir.ActivationFunctionType, mybir.AxisListType

    N, D = x_d.shape
    HEADS = w_d.shape[0]
    TILES = N // P
    PAIRS = TILES // 2
    HALF = 2 * BANK
    QUARTERS = N // HALF
    BLOCKS = BANK // P
    assert D == P and N == UNITS * BANK and QUARTERS * 2 == UNITS

    x_rows = x_d.rearrange("(t p) d -> p t d", p=P)
    adj_tiles = adj_d.rearrange("(t p) m -> p t m", p=P)
    out_tiles = out_d.rearrange("(t p) d -> p t d", p=P)

    ctx = ExitStack()
    with ctx:
        def sb(name, shape, dt):
            return ctx.enter_context(nc.sbuf_tensor(name, shape, dt))

        def ps(name, shape, dt):
            return ctx.enter_context(nc.psum_tensor(name, shape, dt))

        def sem(name):
            return ctx.enter_context(nc.semaphore(name))

        x = sb("x", [P, TILES, D], f32)
        xparts = sb("xparts", [P, TILES, 2 * D], f16)
        xT_hi = sb("xT_hi", [P, N], f16)
        xT_lo = sb("xT_lo", [P, N], f16)
        xwT_hi = sb("xwT_hi", [P, N], f16)
        xwT_lo = sb("xwT_lo", [P, N], f16)
        adj = sb("adj", [P, 2, N], i32)
        mask = sb("mask", [P, 2, HALF], bf16)
        mask_last = sb("mask_last", [P, 2, HALF], bf16)
        relu = sb("relu", [P, 2, HALF], f32)
        probs = sb("probs", [P, 2, N], f32)
        probT_hi = sb("probT_hi", [P, 4, BANK], f16)
        probT_lo = sb("probT_lo", [P, 4, BANK], f16)
        ident = sb("ident", [P, P], f32)
        w_col = sb("w_col", [P, HEADS], f32)
        b_all = sb("b_all", [P, HEADS], f32)
        w_scaled = sb("w_scaled", [P, 1], f32)
        relu_bias = sb("relu_bias", [P, 1], f32)
        chunk_max = sb("chunk_max", [P, 2, QUARTERS], f32)
        row_max = sb("row_max", [P, TILES], f32)
        max_relu = sb("max_relu", [P, 2], f32)
        max_part = sb("max_part", [P, 2], f32)
        max_pad = sb("max_pad", [P, 2], f32)
        max_sum = sb("max_sum", [P, 2], f32)
        shift = sb("shift", [P, 2], f32)
        part_sum = sb("part_sum", [P, 2, QUARTERS], f32)
        scaled_sum = sb("scaled_sum", [P, 2, QUARTERS], f32)
        row_sum = sb("row_sum", [P, 2], f32)
        inv_sum = sb("inv_sum", [P, 2], f32)
        y_hi = sb("y_hi", [P, 2, D], f32)
        y = sb("y", [P, 2, D], f32)
        stats = sb("stats", [P, 2, 6], f32)
        mean_var = sb("mean_var", [P, 2, 2], f32)
        var_eps = sb("var_eps", [P, 2], f32)
        rstd = sb("rstd", [P, 2], f32)
        warm = sb("warm", [P, 1], f32)
        minus_half = sb("minus_half", [P, 1], f32)
        normed = sb("normed", [P, 2, D], f32)
        flag_parts = sb("flag_parts", [P, 2 * QUARTERS + 1], f32)
        flag_scaled = sb("flag_scaled", [P, 2 * QUARTERS + 1], f32)
        flag_row = sb("flag_row", [P, 1], f32)
        flag_max = sb("flag_max", [P, 1], f32)
        flag_word = sb("flag_word", [P, 1], i32)

        score_ps = ps("score_ps", [P, 2, HALF], f32)
        work_ps = ps("work_ps", [P, 4, BANK], f32)
        trans_ps = work_ps[:, 0:3, :]
        mixed_ps = work_ps[:, 3, :]

        x_loaded = [sem(f"x_loaded{c}") for c in range(QUARTERS)]
        w_loaded = sem("w_loaded")
        b_loaded = sem("b_loaded")
        cleared = sem("cleared")
        ident_ready = sem("ident_ready")
        xparts_hi = sem("xparts_hi")
        xparts_ready = sem("xparts_ready")
        xT_ready = sem("xT_ready")
        xT_hi_ready = sem("xT_hi_ready")
        xT_split = sem("xT_split")
        adj_begun = sem("adj_begun")
        bias_ready = sem("bias_ready")
        passed = sem("passed")
        adj_loaded = [sem(f"adj_loaded{s}") for s in range(2)]
        mask_ready = sem("mask_ready")
        mask_last_ready = sem("mask_last_ready")
        scores_ready = sem("scores_ready")
        masked_ready = sem("masked_ready")
        relu_ready = sem("relu_ready")
        leaky_ready = sem("leaky_ready")
        max_kept = sem("max_kept")
        max_part_ready = sem("max_part_ready")
        max_pad_ready = sem("max_pad_ready")
        max_relu_ready = sem("max_relu_ready")
        max_sum_ready = sem("max_sum_ready")
        shift_ready = sem("shift_ready")
        probs_ready = sem("probs_ready")
        transposed = sem("transposed")
        high_ready = sem("high_ready")
        low_ready = sem("low_ready")
        mixed = sem("mixed")
        sum_ready = sem("sum_ready")
        inv_ready = sem("inv_ready")
        y_hi_ready = sem("y_hi_ready")
        y_ready = sem("y_ready")
        stats_ready = sem("stats_ready")
        var_ready = sem("var_ready")
        eps_added = sem("eps_added")
        rstd_ready = sem("rstd_ready")
        norm_ready = sem("norm_ready")
        stored = [sem(f"stored{s}") for s in range(2)]
        flag_step = sem("flag_step")
        flag_local = sem("flag_local")
        flag_step_pool = sem("flag_step_pool")
        flag_ready = sem("flag_ready")
        g_transposed = sem("g_transposed")
        g_xT = sem("g_xT")
        g_adj = sem("g_adj")
        g_xw = sem("g_xw")
        g_scores = sem("g_scores")
        g_dve = sem("g_dve")
        g_alpha = sem("g_alpha")
        g_read = sem("g_read")
        g_probs = sem("g_probs")
        g_probT = sem("g_probT")
        g_copied = sem("g_copied")
        g_mixed = sem("g_mixed")
        g_var = sem("g_var")
        g_pool = sem("g_pool")
        g_norm = sem("g_norm")
        g_stored = sem("g_stored")

        block = ctx.enter_context(nc.Block())

        def back(r, lag):
            return (r - lag) // UNITS, (r - lag) % UNITS

        def exists(tile):
            return not isinstance(tile, int) or 0 <= tile < TILES

        def first(tile, n=1):
            return isinstance(tile, int) and tile < n

        def over_pairs(eng, pair, peeled, drained=2):
            for j in range(peeled):
                pair(j)
            with eng.Fori(peeled, PAIRS) as j:
                pair(j)
            for j in range(PAIRS, PAIRS + drained):
                pair(j)

        def set_up_ps(c):
            return score_ps[:, c, :] if c < 2 else \
                work_ps[:, 2 * c - 4:2 * c - 2, :].rearrange("p a b -> p (a b)")

        def settled(eng):
            eng.sem_inc(passed, 1)

        OWN_MASKS = QUARTERS - 1
        T_LAG = 12
        HI_LAG = T_LAG
        LO_LAG = T_LAG + 1
        MIX_LAG = T_LAG + 2
        EXP_LAG = 10

        @block.sync
        def _(sp):
            n = TILES // QUARTERS
            for c in range(QUARTERS):
                sp.dma_start(x[:, n * c:n * c + n, :], x_rows[:, n * c:n * c + n, :]).then_inc(x_loaded[c], 16)
                if c == 1:
                    sp.dma_start(adj[:, 0, 0:N // 2], adj_tiles[:, 0, 0:N // 2]).then_inc(adj_begun, 16)
            sp.dma_start(adj[:, 0, N // 2:N], adj_tiles[:, 0, N // 2:N]).then_inc(adj_loaded[0], 16)
            sp.dma_start(adj[:, 1, :], adj_tiles[:, 1, :]).then_inc(adj_loaded[1], 16)

            STORE_LAG = 5

            def pair(j):
                for s in range(2):
                    i = 2 * j + s
                    if exists(i) and not first(i, 2):
                        sp.wait_ge(mask_ready, OWN_MASKS * (i - 1))
                        sp.wait_ge(mask_last_ready, i - 1)
                        sp.dma_start(adj[:, s, :], adj_tiles[:, bass.ds(i, 1), :]).then_inc(adj_loaded[s], 16)
                    k = i - STORE_LAG
                    if exists(k):
                        store(k, 1 - s)

            def store(k, s):
                sp.wait_ge(norm_ready, k + 1)
                sp.dma_start(out_tiles[:, bass.ds(k, 1), :], normed[:, s, :]).then_inc(stored[s], 16)

            over_pairs(sp, pair, peeled=3, drained=3)
            for s in range(2):
                sp.wait_ge(stored[s], 16 * PAIRS)

            sp.wait_ge(flag_ready, 1)
            general = sp.value_load(flag_word[0:1, 0:1], min_val=0, max_val=1)
            with sp.If(general > 0):
                with sp.Fori(0, TILES) as t:
                    sp.dma_start(adj[:, 0, :], adj_tiles[:, bass.ds(t, 1), :]).then_inc(g_adj, 16)
                    sp.wait_ge(g_norm, t + 1)
                    sp.dma_start(out_tiles[:, bass.ds(t, 1), :], normed[:, 0, :]).then_inc(g_stored, 16)
                sp.wait_ge(g_stored, 16 * TILES)
            sp.nop()

        @block.gpsimd
        def _(pool):
            nc.gpsimd.memset(ident[:, :], 0.0).then_inc(cleared, 1)
            nc.gpsimd.memset(minus_half[:, :], -0.5).then_inc(cleared, 1)
            pool.wait_ge(cleared, 2)
            nc.gpsimd.affine_select(out=ident[:, :], in_=ident[:, :], compare_op=ALU.not_equal, fill=1.0, base=0,
                                    pattern=[[-1, P]], channel_multiplier=1).then_inc(ident_ready, 1)

            def make_mask(i, s):
                pool.wait_ge(adj_loaded[s], 8 * (i - s) + 16)
                if not first(i, 2):
                    pool.wait_ge(masked_ready, QUARTERS * i - QUARTERS)
                settled(pool)
                nc.gpsimd.tensor_scalar(mask_last[:, s, :], adj[:, s, N - HALF:N], -1.0, BIG,
                                        ALU.add, ALU.mult).then_inc(mask_last_ready, 1)

            def leaky(i, s, c):
                q = QUARTERS * i + c
                part = probs[:, s, HALF * c:HALF * c + HALF]
                pool.wait_ge(relu_ready, q + 1)
                nc.gpsimd.tensor_tensor(part, part, relu[:, c % 2, :], ALU.add).then_inc(leaky_ready, 1)

            def layer_norm(i, s):
                pool.wait_ge(var_ready, i + 1)
                settled(pool)
                nc.gpsimd.tensor_scalar(var_eps[:, s:s + 1], mean_var[:, s, 1:2], EPS, None,
                                        ALU.add).then_inc(eps_added, 1)
                pool.wait_ge(eps_added, i + 1)
                nc.gpsimd.tensor_tensor(rstd[:, s:s + 1], var_eps[:, s:s + 1], minus_half[:, :],
                                        ALU.pow).then_inc(rstd_ready, 1)
                pool.wait_ge(rstd_ready, i + 1)
                if not first(i, 2):
                    pool.wait_ge(stored[s], 8 * (i - s))
                settled(pool)
                nc.gpsimd.tensor_scalar(normed[:, s, :], y[:, s, :], mean_var[:, s, 0:1], rstd[:, s:s + 1],
                                        ALU.subtract, ALU.mult).then_inc(norm_ready, 1)

            make_mask(0, 0)

            def pair(j):
                for s in range(2):
                    i = 2 * j + s
                    for c in range(QUARTERS):
                        if exists(i):
                            leaky(i, s, c)
                        if exists(i) and c == QUARTERS - 1:
                            nc.gpsimd.tensor_copy(row_max[:, bass.ds(i, 1)],
                                                  chunk_max[:, s, QUARTERS - 1:QUARTERS]).then_inc(max_kept, 1)
                        if c == 1 and exists(i - 3):
                            layer_norm(i - 3, 1 - s)
                        if c == 1 and exists(i + 1):
                            make_mask(i + 1, 1 - s)

            for j in range(3):
                pair(j)
            with pool.Fori(3, PAIRS - 1) as j:
                pair(j)
            for j in range(PAIRS - 1, PAIRS + 1):
                pair(j)

            pool.wait_ge(flag_local, 1)
            nc.gpsimd.partition_all_reduce(flag_max[:, :], flag_row[:, :], P,
                                           bass.bass_isa.ReduceOp.max).then_inc(flag_step_pool, 1)
            pool.wait_ge(flag_step_pool, 1)
            nc.gpsimd.tensor_scalar(flag_word[:, :], flag_max[:, :], 1.0, None, ALU.is_gt).then_inc(flag_ready, 1)
            layer_norm(TILES - 1, 1)
            pool.wait_ge(flag_ready, 1)
            general = pool.value_load(flag_word[0:1, 0:1], min_val=0, max_val=1)
            with pool.If(general > 0):
                for s in range(2):
                    pool.wait_ge(stored[s], 16 * PAIRS)
                with pool.Fori(0, TILES) as t:
                    pool.wait_ge(g_var, t + 1)
                    settled(pool)
                    nc.gpsimd.tensor_scalar(var_eps[:, 0:1], mean_var[:, 0, 1:2], EPS, None,
                                            ALU.add).then_inc(g_pool, 1)
                    pool.wait_ge(g_pool, 2 * t + 1)
                    nc.gpsimd.tensor_tensor(rstd[:, 0:1], var_eps[:, 0:1], minus_half[:, :],
                                            ALU.pow).then_inc(g_pool, 1)
                    pool.wait_ge(g_pool, 2 * t + 2)
                    settled(pool)
                    nc.gpsimd.tensor_scalar(normed[:, 0, :], y[:, 0, :], mean_var[:, 0, 0:1], rstd[:, 0:1],
                                            ALU.subtract, ALU.mult).then_inc(g_norm, 1)
                    pool.wait_ge(g_stored, 16 * t + 16)
            pool.nop()

        @block.tensor
        def _(pe):
            pe.wait_ge(ident_ready, 1)
            for c in range(QUARTERS):
                pe.wait_ge(x_loaded[c], 16)
                for k in range(HALF // P):
                    last = nc.tensor.transpose(set_up_ps(c)[:, P * k:P * k + P], x[:, HALF // P * c + k, :],
                                               ident[:, :])
                last.then_inc(xT_ready, 1)

            def scores(j, r):
                off, u = back(r, 0)
                i = 2 * j + off
                if not exists(i):
                    return
                c, h = u // 2, u % 2
                if isinstance(j, int) and j == 0 and off == 0 and h == 0:
                    pe.wait_ge(xT_split, c + 1)
                if h == 0 and not (isinstance(i, int) and QUARTERS * i + c < 2):
                    pe.wait_ge(masked_ready, QUARTERS * i + c - 1)
                out = score_ps[:, c % 2, h * BANK:h * BANK + BANK]
                cols = slice(u * BANK, u * BANK + BANK)
                rows = bass.ds(P * i, P)
                nc.tensor.matmul(out, xwT_hi[:, rows], xT_hi[:, cols], start=True, stop=False)
                nc.tensor.matmul(out, xwT_hi[:, rows], xT_lo[:, cols], start=False, stop=False)
                nc.tensor.matmul(out, xwT_lo[:, rows], xT_hi[:, cols], start=False, stop=True)\
                    .then_inc(scores_ready, 1)

            def transposes(j, r):
                off, g = back(r, T_LAG)
                i = 2 * j + off
                if not exists(i):
                    return
                if g % 2 == 0:
                    pe.wait_ge(probs_ready, QUARTERS * i + g // 2 + 1)
                if g >= 3 or not first(i):
                    pe.wait_ge(low_ready, UNITS * i + g - (2 if g >= 3 else 4 if g == 2 else 1))
                for k in range(BLOCKS):
                    m = g * BANK + k * P
                    last = nc.tensor.transpose(trans_ps[:, g % 3, P * k:P * k + P], probs[:, off % 2, m:m + P],
                                               ident[:, :])
                last.then_inc(transposed, 1)

            def mix(j, r):
                off, g = back(r, MIX_LAG)
                i = 2 * j + off
                if not exists(i) or g == 0:
                    return
                if g == 1:
                    if first(i):
                        pe.wait_ge(xparts_ready, QUARTERS)
                    else:
                        pe.wait_ge(y_ready, i)
                    mix_unit(i, 0)
                mix_unit(i, g)

            def mix_unit(i, g):
                pe.wait_ge(low_ready, UNITS * i + g + 1)
                for k in range(BLOCKS):
                    m = g * BLOCKS + k
                    hi = probT_hi[:, g % 4, P * k:P * k + P]
                    lo = probT_lo[:, g % 4, P * k:P * k + P]
                    nc.tensor.matmul(mixed_ps[:, 0:2 * D], hi, xparts[:, m, :], start=(m == 0), stop=False,
                                     skip_group_check=True)
                    last = nc.tensor.matmul(mixed_ps[:, 0:D], lo, xparts[:, m, 0:D], start=False,
                                            stop=(m == TILES - 1), skip_group_check=True)
                last.then_inc(mixed, 1)

            def pair(j):
                for r in range(2 * UNITS):
                    scores(j, r)
                    transposes(j, r)
                    mix(j, r)

            over_pairs(pe, pair, peeled=2)

            pe.wait_ge(flag_ready, 1)
            general = pe.value_load(flag_word[0:1, 0:1], min_val=0, max_val=1)
            with pe.If(general > 0):
                for c in range(QUARTERS):
                    if c >= 2:
                        pe.wait_ge(g_xT, c - 1)
                    for k in range(HALF // P):
                        last = nc.tensor.transpose(score_ps[:, c % 2, P * k:P * k + P],
                                                   x[:, HALF // P * c + k, :], ident[:, :])
                    last.then_inc(g_transposed, 1)
                pe.wait_ge(g_xT, QUARTERS)
                with pe.Fori(0, TILES) as t:
                    pe.wait_ge(g_xw, t + 1)
                    for n in range(HEADS * UNITS):
                        u, k = n // HEADS, n % HEADS
                        if n >= 2:
                            pe.wait_ge(g_read, HEADS * UNITS * t + n - 1)
                        nc.tensor.matmul(score_ps[:, n % 2, 0:BANK], relu[:, 0, P * k:P * k + P],
                                         probs[:, 1, u * BANK:u * BANK + BANK], start=True, stop=True)\
                            .then_inc(g_scores, 1)
                    pe.wait_ge(g_probs, t + 1)
                    for g in range(UNITS):
                        for k in range(BLOCKS):
                            m = g * BANK + k * P
                            last = nc.tensor.transpose(trans_ps[:, 0, P * k:P * k + P], probs[:, 0, m:m + P],
                                                       ident[:, :])
                        last.then_inc(g_probT, 1)
                        pe.wait_ge(g_copied, UNITS * t + g + 1)
                        for k in range(BLOCKS):
                            m = g * BLOCKS + k
                            last = nc.tensor.matmul(mixed_ps[:, 0:D], relu[:, 1, P * k:P * k + P],
                                                    x[:, m, :], start=(m == 0), stop=(m == TILES - 1))
                        last.then_inc(g_mixed, 1)
            pe.nop()

        @block.scalar
        def _(act):
            act.dma_start(w_col[:, :], w_d.rearrange("k d -> d k"), allow_slow_non_contiguous=True).then_inc(w_loaded, 16)
            act.dma_start(b_all[:, :], b_d.rearrange("(a k) -> a k", a=1).broadcast_to([P, HEADS]))\
                .then_inc(b_loaded, 16)
            act.wait_ge(cleared, 2)
            nc.scalar.activation(warm[:, :], minus_half[:, :], ACT.Exp)
            for c in range(QUARTERS):
                cols = slice(HALF * c, HALF * c + HALF)
                act.wait_ge(xT_ready, c + 1)
                nc.scalar.activation(xT_hi[:, cols], set_up_ps(c), ACT.Copy, scale=X_SCALE).then_inc(xT_hi_ready, 1)
                if c == 0:
                    act.wait_ge(bias_ready, 2)
                nc.scalar.activation(xwT_hi[:, cols], set_up_ps(c), ACT.Copy, scale=w_scaled[:, :])\
                    .then_inc(xT_hi_ready, 1)
            for c in range(QUARTERS):
                rows = slice(TILES // QUARTERS * c, TILES // QUARTERS * (c + 1))
                act.wait_ge(x_loaded[c], 16)
                nc.scalar.activation(xparts[:, rows, 0:D], x[:, rows, :], ACT.Copy, scale=X_SCALE)\
                    .then_inc(xparts_hi, 1)

            def do_relu(j, r):
                off, u = back(r, 3)
                i = 2 * j + off
                if u % 2 or not exists(i):
                    return
                q = QUARTERS * i + u // 2
                c = u // 2
                act.wait_ge(masked_ready, q + 1)
                if not (isinstance(q, int) and q < 2):
                    act.wait_ge(leaky_ready, q - 1)
                nc.scalar.activation(relu[:, c % 2, :], probs[:, off % 2, HALF * c:HALF * c + HALF], ACT.Relu,
                                     bias=relu_bias[:, :], scale=1.0 / SLOPE - 1.0).then_inc(relu_ready, 1)

            def do_exp(j, r):
                off, u = back(r, EXP_LAG)
                i = 2 * j + off
                if u % 2 or not exists(i):
                    return
                s, c = off % 2, u // 2
                if c == 0:
                    act.wait_ge(shift_ready, i + 1)
                    if not first(i, 2):
                        act.wait_ge(sum_ready, i - 1)
                act.wait_ge(leaky_ready, QUARTERS * i + c + 1)
                part = probs[:, s, HALF * c:HALF * c + HALF]
                nc.scalar.activation(part, part, ACT.Exp, bias=shift[:, s:s + 1], scale=SLOPE / SCORE_SCALE,
                                     accum_out=part_sum[:, s, c:c + 1]).then_inc(probs_ready, 1)

            def do_high(j, r):
                off, g = back(r, HI_LAG)
                i = 2 * j + off
                if not exists(i):
                    return
                act.wait_ge(transposed, UNITS * i + g + 1)
                if not (isinstance(i, int) and UNITS * i + g < 4):
                    act.wait_ge(mixed, UNITS * i + g - 3)
                nc.scalar.activation(probT_hi[:, g % 4, :], trans_ps[:, g % 3, :], ACT.Copy,
                                     scale=PROB_SCALE).then_inc(high_ready, 1)

            def pair(j):
                for r in range(2 * UNITS):
                    do_high(j, r)
                    do_relu(j, r)
                    do_exp(j, r)

            over_pairs(act, pair, peeled=2)

            act.wait_ge(flag_ready, 1)
            general = act.value_load(flag_word[0:1, 0:1], min_val=0, max_val=1)
            with act.If(general > 0):
                for c in range(QUARTERS):
                    act.wait_ge(g_transposed, c + 1)
                    nc.scalar.activation(probs[:, 1, HALF * c:HALF * c + HALF], score_ps[:, c % 2, :],
                                         ACT.Copy).then_inc(g_xT, 1)
                with act.Fori(0, TILES) as t:
                    act.wait_ge(g_alpha, t + 1)
                    nc.scalar.activation(probs[:, 0, :], probs[:, 0, :], ACT.Exp, bias=shift[:, 0:1],
                                         accum_out=part_sum[:, 0, 0:1]).then_inc(g_probs, 1)
                    for g in range(UNITS):
                        act.wait_ge(g_probT, UNITS * t + g + 1)
                        if g:
                            act.wait_ge(g_mixed, UNITS * t + g)
                        nc.scalar.activation(relu[:, 1, 0:BANK], trans_ps[:, 0, :], ACT.Copy).then_inc(g_copied, 1)
            act.nop()

        @block.vector
        def _(dve):
            dve.wait_ge(w_loaded, 16)
            nc.vector.tensor_scalar(w_scaled[:, :], w_col[:, 0:1], XW_SCALE, None, ALU.mult).then_inc(bias_ready, 1)
            dve.wait_ge(b_loaded, 16)
            nc.vector.tensor_scalar(relu_bias[:, :], b_all[:, 0:1], (1.0 / SLOPE - 1.0) * SCORE_SCALE, None,
                                    ALU.mult).then_inc(bias_ready, 1)
            dve.wait_ge(bias_ready, 2)

            def split(c):
                cols = slice(HALF * c, HALF * c + HALF)
                dve.wait_ge(xT_hi_ready, 2 * c + 2)
                nc.vector.scalar_tensor_tensor(out=xT_lo[:, cols], in0=set_up_ps(c), scalar=X_SCALE,
                                               in1=xT_hi[:, cols], op0=ALU.mult, op1=ALU.subtract)
                nc.vector.scalar_tensor_tensor(out=xwT_lo[:, cols], in0=set_up_ps(c), scalar=w_scaled[:, :],
                                               in1=xwT_hi[:, cols], op0=ALU.mult, op1=ALU.subtract)\
                    .then_inc(xT_split, 1)

            split(0)
            split(1)

            def do_x_low(c):
                rows = slice(TILES // QUARTERS * c, TILES // QUARTERS * (c + 1))
                dve.wait_ge(xparts_hi, c + 1)
                nc.vector.scalar_tensor_tensor(out=xparts[:, rows, D:2 * D], in0=x[:, rows, :], scalar=X_SCALE,
                                               in1=xparts[:, rows, 0:D], op0=ALU.mult, op1=ALU.subtract)\
                    .then_inc(xparts_ready, 1)

            def do_low(j, r):
                off, g = back(r, LO_LAG)
                i = 2 * j + off
                if not exists(i):
                    return
                dve.wait_ge(high_ready, UNITS * i + g + 1)
                if not (isinstance(i, int) and UNITS * i + g < 4):
                    dve.wait_ge(mixed, UNITS * i + g - 3)
                nc.vector.scalar_tensor_tensor(out=probT_lo[:, g % 4, :], in0=trans_ps[:, g % 3, :], scalar=PROB_SCALE,
                                               in1=probT_hi[:, g % 4, :], op0=ALU.mult, op1=ALU.subtract)\
                    .then_inc(low_ready, 1)

            def do_mask(j, r):
                off, u = back(r, 1)
                i = 2 * j + off
                if u % 2 or not exists(i):
                    return
                c, s = u // 2, off % 2
                if c == OWN_MASKS:
                    return
                if first(i) and c == 0:
                    dve.wait_ge(adj_begun, 16)
                elif first(i) and c == 2 or not first(i) and c == 0:
                    dve.wait_ge(adj_loaded[s], 8 * (i - s) + 16)
                if not first(i) or c == 2:
                    dve.wait_ge(masked_ready, QUARTERS * i + (-1, -2, 1)[c])
                nc.vector.tensor_scalar(mask[:, c % 2, :], adj[:, s, HALF * c:HALF * c + HALF], -1.0, BIG,
                                        ALU.add, ALU.mult).then_inc(mask_ready, 1)

            def do_masked(j, r):
                off, u = back(r, 2)
                i = 2 * j + off
                if u % 2 or not exists(i):
                    return
                c, s = u // 2, off % 2
                q = QUARTERS * i + c
                if c < OWN_MASKS:
                    dve.wait_ge(mask_ready, OWN_MASKS * i + c + 1)
                else:
                    dve.wait_ge(mask_last_ready, i + 1)
                if not first(i, 2):
                    dve.wait_ge(transposed, UNITS * i - 2 * UNITS + 2 * c + 2)
                dve.wait_ge(scores_ready, 2 * q + 2)
                if c:
                    dve.wait_ge(masked_ready, q)
                elif not first(i, 2):
                    dve.wait_ge(max_kept, i - 1)
                settled(dve)
                nc.vector.tensor_tensor_reduce(
                    out=probs[:, s, HALF * c:HALF * c + HALF], in0=score_ps[:, c % 2, :],
                    in1=mask[:, c % 2, :] if c < OWN_MASKS else mask_last[:, s, :],
                    scale=1.0, scalar=chunk_max[:, s, c - 1:c] if c else -3e38, op0=ALU.add, op1=ALU.max,
                    accum_out=chunk_max[:, s, c:c + 1]).then_inc(masked_ready, 1)

            def do_max(j, r, step):
                off, u = back(r, (8, 9, 9)[step])
                i = 2 * j + off
                if u or not exists(i):
                    return
                s = off % 2
                m = chunk_max[:, s, QUARTERS - 1:QUARTERS]
                if step == 0:
                    dve.wait_ge(masked_ready, QUARTERS * i + QUARTERS)
                    nc.vector.tensor_scalar(max_part[:, s:s + 1], m, PAD / SCORE_SCALE, None,
                                            ALU.mult).then_inc(max_part_ready, 1)
                    nc.vector.tensor_scalar(max_relu[:, s:s + 1], m, 1.0 / SLOPE - 1.0, relu_bias[:, :],
                                            ALU.mult, ALU.add).then_inc(max_relu_ready, 1)
                    dve.wait_ge(max_part_ready, i + 1)
                    nc.vector.scalar_tensor_tensor(out=max_pad[:, s:s + 1], in0=m, scalar=-PAD / SCORE_SCALE,
                                                   in1=max_part[:, s:s + 1], op0=ALU.mult, op1=ALU.max)\
                        .then_inc(max_pad_ready, 1)
                elif step == 1:
                    dve.wait_ge(max_relu_ready, i + 1)
                    nc.vector.scalar_tensor_tensor(out=max_sum[:, s:s + 1], in0=max_relu[:, s:s + 1], scalar=0.0,
                                                   in1=m, op0=ALU.max, op1=ALU.add).then_inc(max_sum_ready, 1)
                else:
                    dve.wait_ge(max_sum_ready, i + 1)
                    dve.wait_ge(max_pad_ready, i + 1)
                    nc.vector.scalar_tensor_tensor(out=shift[:, s:s + 1], in0=max_sum[:, s:s + 1],
                                                   scalar=-SLOPE / SCORE_SCALE, in1=max_pad[:, s:s + 1],
                                                   op0=ALU.mult, op1=ALU.subtract).then_inc(shift_ready, 1)

            def do_tail(j, r, step):
                off, u = back(r, (18, 19, 22, 22, 23, 24)[step])
                i = 2 * j + off
                if u or not exists(i):
                    return
                s = off % 2
                if step == 0:
                    dve.wait_ge(probs_ready, QUARTERS * i + QUARTERS)
                    nc.vector.tensor_scalar(scaled_sum[:, s, :], part_sum[:, s, :], X_SCALE * PROB_SCALE, TINY_SUM,
                                            ALU.mult, ALU.add, accum_out=row_sum[:, s:s + 1]).then_inc(sum_ready, 1)
                elif step == 1:
                    dve.wait_ge(sum_ready, i + 1)
                    nc.vector.reciprocal(inv_sum[:, s:s + 1], row_sum[:, s:s + 1]).then_inc(inv_ready, 1)
                elif step == 2:
                    dve.wait_ge(inv_ready, i + 1)
                    dve.wait_ge(mixed, UNITS * i + UNITS)
                    nc.vector.scalar_tensor_tensor(out=y_hi[:, s, :], in0=mixed_ps[:, 0:D],
                                                   scalar=inv_sum[:, s:s + 1],
                                                   in1=x[:, bass.ds(i, 1), :].rearrange("p a d -> p (a d)"),
                                                   op0=ALU.mult, op1=ALU.add).then_inc(y_hi_ready, 1)
                elif step == 3:
                    dve.wait_ge(y_hi_ready, i + 1)
                    if not first(i, 2):
                        dve.wait_ge(norm_ready, i - 1)
                    nc.vector.scalar_tensor_tensor(out=y[:, s, :], in0=mixed_ps[:, D:2 * D],
                                                   scalar=inv_sum[:, s:s + 1], in1=y_hi[:, s, :],
                                                   op0=ALU.mult, op1=ALU.add).then_inc(y_ready, 1)
                elif step == 4:
                    dve.wait_ge(y_ready, i + 1)
                    nc.vector.bn_stats(stats[:, s, :], y[:, s, :]).then_inc(stats_ready, 1)
                else:
                    dve.wait_ge(stats_ready, i + 1)
                    settled(dve)
                    nc.vector.bn_aggr(mean_var[:, s, :], stats[:, s, :]).then_inc(var_ready, 1)

            def do_range_flag(n):
                part = (xT_hi, xwT_hi)[n // QUARTERS][:, HALF * (n % QUARTERS):HALF * (n % QUARTERS) + HALF]
                nc.vector.tensor_reduce(flag_parts[:, n:n + 1], part, AX.X, ALU.max,
                                        apply_absolute_value=True).then_inc(flag_step, 1)

            def do_flags():
                n = 2 * QUARTERS
                dve.wait_ge(max_kept, TILES)
                nc.vector.tensor_reduce(flag_parts[:, n:n + 1], row_max[:, :], AX.X, ALU.max,
                                        apply_absolute_value=True).then_inc(flag_step, 1)
                dve.wait_ge(flag_step, n + 1)
                nc.vector.tensor_scalar(flag_scaled[:, 0:n], flag_parts[:, 0:n], 1.0 / FLAG_PART, None,
                                        ALU.mult).then_inc(flag_step, 1)
                nc.vector.tensor_scalar(flag_scaled[:, n:n + 1], flag_parts[:, n:n + 1], 1.0 / FLAG_SCORE, None,
                                        ALU.mult).then_inc(flag_step, 1)
                dve.wait_ge(flag_step, n + 3)
                nc.vector.tensor_reduce(flag_row[:, :], flag_scaled[:, :], AX.X, ALU.max).then_inc(flag_local, 1)

            def pair(j):
                for r in range(2 * UNITS):
                    do_tail(j, r, 2)
                    do_low(j, r)
                    do_tail(j, r, 3)
                    do_tail(j, r, 4)
                    do_tail(j, r, 5)
                    do_max(j, r, 1)
                    do_mask(j, r)
                    do_masked(j, r)
                    do_max(j, r, 2)
                    do_tail(j, r, 0)
                    do_tail(j, r, 1)
                    if isinstance(j, int) and j == 0 and r in (1, 2):
                        split(r + 1)
                    if isinstance(j, int) and j == 0 and r in (5, 7, 9, 11):
                        do_x_low((r - 5) // 2)
                    if isinstance(j, int) and j == 1 and r % 2 == 1:
                        do_range_flag(r // 2)
                    if isinstance(j, int) and j == PAIRS and r == 3:
                        do_flags()
                    do_max(j, r, 0)

            over_pairs(dve, pair, peeled=2)

            dve.wait_ge(flag_ready, 1)
            general = dve.value_load(flag_word[0:1, 0:1], min_val=0, max_val=1)
            with dve.If(general > 0):
                dve.wait_ge(norm_ready, TILES)
                STEPS = HEADS + UNITS * (3 + 3 * HEADS) + 4
                with dve.Fori(0, TILES) as t:
                    done = 0

                    def own(instruction):
                        nonlocal done
                        done += 1
                        instruction.then_inc(g_dve, 1)
                        dve.wait_ge(g_dve, STEPS * t + done)

                    dve.wait_ge(g_xT, QUARTERS)
                    dve.wait_ge(g_adj, 16 * t + 16)
                    for k in range(HEADS):
                        own(nc.vector.tensor_scalar(relu[:, 0, P * k:P * k + P],
                                                    probs[:, 1, bass.ds(P * t, P)],
                                                    w_col[:, k:k + 1], None, ALU.mult))
                    nc.vector.tensor_copy(row_sum[:, 1:2], row_sum[:, 0:1]).then_inc(g_xw, 1)
                    for u in range(UNITS):
                        cols = slice(u * BANK, u * BANK + BANK)
                        alpha, a = probs[:, 0, cols], adj[:, 0, cols]
                        tmp = [adj[:, 1, n * BANK:n * BANK + BANK].bitcast(f32) for n in range(3)]
                        own(nc.vector.tensor_scalar(tmp[0], a, 1.0, NEG, ALU.is_lt, ALU.mult))
                        own(nc.vector.tensor_scalar(tmp[1], a, float(HEADS), NEG, ALU.is_gt, ALU.mult))
                        own(nc.vector.tensor_tensor(alpha, tmp[0], tmp[1], ALU.add))
                        for k in range(HEADS):
                            n = HEADS * u + k
                            dve.wait_ge(g_scores, HEADS * UNITS * t + n + 1)
                            nc.vector.tensor_scalar(tmp[0], score_ps[:, n % 2, 0:BANK], b_all[:, k:k + 1], None,
                                                    ALU.add).then_inc(g_read, 1)
                            dve.wait_ge(g_read, HEADS * UNITS * t + n + 1)
                            own(nc.vector.scalar_tensor_tensor(out=tmp[1], in0=tmp[0], scalar=SLOPE, in1=tmp[0],
                                                               op0=ALU.mult, op1=ALU.max))
                            own(nc.vector.scalar_tensor_tensor(out=tmp[2], in0=a, scalar=float(k + 1), in1=tmp[1],
                                                               op0=ALU.is_equal, op1=ALU.mult))
                            own(nc.vector.tensor_tensor(alpha, alpha, tmp[2], ALU.add))
                    own(nc.vector.tensor_reduce(chunk_max[:, 0, 0:1], probs[:, 0, :], AX.X, ALU.max))
                    nc.vector.tensor_scalar(shift[:, 0:1], chunk_max[:, 0, 0:1], -1.0, None,
                                            ALU.mult).then_inc(g_alpha, 1)
                    dve.wait_ge(g_probs, t + 1)
                    own(nc.vector.reciprocal(inv_sum[:, 0:1], part_sum[:, 0, 0:1]))
                    dve.wait_ge(g_mixed, UNITS * t + UNITS)
                    own(nc.vector.scalar_tensor_tensor(out=y[:, 0, :], in0=mixed_ps[:, 0:D],
                                                       scalar=inv_sum[:, 0:1],
                                                       in1=x[:, bass.ds(t, 1), :].rearrange("p a d -> p (a d)"),
                                                       op0=ALU.mult, op1=ALU.add))
                    own(nc.vector.bn_stats(stats[:, 0, :], y[:, 0, :]))
                    settled(dve)
                    nc.vector.bn_aggr(mean_var[:, 0, :], stats[:, 0, :]).then_inc(g_var, 1)
                    dve.wait_ge(g_norm, t + 1)
                    STEPS_USED = done
                assert STEPS_USED == HEADS + UNITS * (3 + 3 * HEADS) + 4, STEPS_USED
            dve.nop()


_INS = ["x", "adj", "L0_gnn_W", "L0_gnn_b"]


def kernel(**inputs):
    import numpy as np
    import concourse.bacc as bacc
    from concourse import mybir as mb
    from concourse.bass_utils import run_bass_kernel_spmd

    nc = bacc.Bacc("TRN2", target_bir_lowering=False, num_devices=1)
    arrays, args = {}, []
    for name in _INS:
        a = np.ascontiguousarray(inputs[name])
        arrays[f"in_{name}"] = a
        args.append(nc.dram_tensor(f"in_{name}", a.shape, mb.dt.from_np(a.dtype), kind="ExternalInput").ap())
    out = nc.dram_tensor("out", inputs["x"].shape, mb.dt.float32, kind="ExternalOutput").ap()
    graph_attention(nc, *args, out)
    return run_bass_kernel_spmd(nc, [arrays], core_ids=[0]).results[0]["out"]
```

```python
import concourse.bass as bass
from concourse import mybir
from contextlib import ExitStack

P = 128
BANK = 512
SLOPE = 0.2
EPS = 1e-5
NEG = -9000000000000000.0
BIG = 2.0 ** 63
X_SCALE = 16.0
XW_SCALE = 64.0
PROB_SCALE = 4096.0
SCORE_SCALE = X_SCALE * XW_SCALE
PAD = 2.0 ** -20
TINY_SUM = 1e-30
FLAG_SCORE = 1e15
FLAG_PART = 32768.0
UNITS = 8


def graph_attention(nc, x_d, adj_d, w_d, b_d, out_d):
    f32, f16, bf16, i32 = mybir.dt.float32, mybir.dt.float16, mybir.dt.bfloat16, mybir.dt.int32
    ALU, ACT, AX = mybir.AluOpType, mybir.ActivationFunctionType, mybir.AxisListType

    N, D = x_d.shape
    HEADS = w_d.shape[0]
    TILES = N // P
    PAIRS = TILES // 2
    HALF = 2 * BANK
    QUARTERS = N // HALF
    BLOCKS = BANK // P
    assert D == P and N == UNITS * BANK and QUARTERS * 2 == UNITS

    x_rows = x_d.rearrange("(t p) d -> p t d", p=P)
    adj_tiles = adj_d.rearrange("(t p) m -> p t m", p=P)
    out_tiles = out_d.rearrange("(t p) d -> p t d", p=P)

    ctx = ExitStack()
    with ctx:
        def sb(name, shape, dt):
            return ctx.enter_context(nc.sbuf_tensor(name, shape, dt))

        def ps(name, shape, dt):
            return ctx.enter_context(nc.psum_tensor(name, shape, dt))

        def sem(name):
            return ctx.enter_context(nc.semaphore(name))

        x = sb("x", [P, TILES, D], f32)
        xparts = sb("xparts", [P, TILES, 2 * D], f16)
        xwT_scaled = sb("xwT_scaled", [P, N], f32)
        xT_hi = sb("xT_hi", [P, N], f16)
        xT_lo = sb("xT_lo", [P, N], f16)
        xwT_hi = sb("xwT_hi", [P, N], f16)
        xwT_lo = sb("xwT_lo", [P, N], f16)
        adj = sb("adj", [P, 2, N], i32)
        mask = sb("mask", [P, 2, HALF], bf16)
        mask_last = sb("mask_last", [P, 2, HALF], bf16)
        relu = sb("relu", [P, 2, HALF], f32)
        probs = sb("probs", [P, 2, N], f32)
        probT_hi = sb("probT_hi", [P, 4, BANK], f16)
        probT_lo = sb("probT_lo", [P, 4, BANK], f16)
        ident = sb("ident", [P, P], f32)
        w_col = sb("w_col", [P, HEADS], f32)
        b_all = sb("b_all", [P, HEADS], f32)
        w_scaled = sb("w_scaled", [P, 1], f32)
        relu_bias = sb("relu_bias", [P, 1], f32)
        chunk_max = sb("chunk_max", [P, 2, QUARTERS], f32)
        row_max = sb("row_max", [P, TILES], f32)
        max_relu = sb("max_relu", [P, 2], f32)
        max_part = sb("max_part", [P, 2], f32)
        max_pad = sb("max_pad", [P, 2], f32)
        max_sum = sb("max_sum", [P, 2], f32)
        shift = sb("shift", [P, 2], f32)
        part_sum = sb("part_sum", [P, 2, QUARTERS], f32)
        scaled_sum = sb("scaled_sum", [P, 2, QUARTERS], f32)
        row_sum = sb("row_sum", [P, 2], f32)
        inv_sum = sb("inv_sum", [P, 2], f32)
        y_hi = sb("y_hi", [P, 2, D], f32)
        y = sb("y", [P, 2, D], f32)
        stats = sb("stats", [P, 2, 6], f32)
        mean_var = sb("mean_var", [P, 2, 2], f32)
        var_eps = sb("var_eps", [P, 2], f32)
        rstd = sb("rstd", [P, 2], f32)
        warm = sb("warm", [P, 1], f32)
        minus_half = sb("minus_half", [P, 1], f32)
        normed = sb("normed", [P, 2, D], f32)
        flag_parts = sb("flag_parts", [P, 2 * PAIRS + 1], f32)
        flag_scaled = sb("flag_scaled", [P, 2 * PAIRS + 1], f32)
        flag_row = sb("flag_row", [P, 1], f32)
        flag_max = sb("flag_max", [P, 1], f32)
        flag_word = sb("flag_word", [P, 1], i32)

        score_ps = ps("score_ps", [P, 2, HALF], f32)
        work_ps = ps("work_ps", [P, 4, BANK], f32)
        trans_ps = work_ps[:, 0:3, :]
        mixed_ps = work_ps[:, 3, :]

        x_loaded = [sem(f"x_loaded{c}") for c in range(QUARTERS)]
        w_loaded = sem("w_loaded")
        b_loaded = sem("b_loaded")
        cleared = sem("cleared")
        ident_ready = sem("ident_ready")
        xparts_hi = sem("xparts_hi")
        xparts_ready = sem("xparts_ready")
        xT_ready = sem("xT_ready")
        xT_hi_ready = sem("xT_hi_ready")
        xT_split = sem("xT_split")
        xwT_hi_begun = sem("xwT_hi_begun")
        xwT_begun = sem("xwT_begun")
        xwT_kept = sem("xwT_kept")
        xwT_hi_ready = sem("xwT_hi_ready")
        xwT_split = sem("xwT_split")
        adj_begun = sem("adj_begun")
        bias_ready = sem("bias_ready")
        passed = sem("passed")
        adj_loaded = [sem(f"adj_loaded{s}") for s in range(2)]
        mask_ready = sem("mask_ready")
        mask_last_ready = sem("mask_last_ready")
        scores_ready = sem("scores_ready")
        masked_ready = sem("masked_ready")
        relu_ready = sem("relu_ready")
        leaky_ready = sem("leaky_ready")
        max_kept = sem("max_kept")
        max_part_ready = sem("max_part_ready")
        max_pad_ready = sem("max_pad_ready")
        max_relu_ready = sem("max_relu_ready")
        max_sum_ready = sem("max_sum_ready")
        shift_ready = sem("shift_ready")
        probs_ready = sem("probs_ready")
        transposed = sem("transposed")
        high_ready = sem("high_ready")
        low_ready = sem("low_ready")
        mixed = sem("mixed")
        sum_ready = sem("sum_ready")
        inv_ready = sem("inv_ready")
        y_hi_ready = sem("y_hi_ready")
        y_ready = sem("y_ready")
        stats_ready = sem("stats_ready")
        var_ready = sem("var_ready")
        eps_added = sem("eps_added")
        rstd_ready = sem("rstd_ready")
        norm_ready = sem("norm_ready")
        stored = [sem(f"stored{s}") for s in range(2)]
        flag_step = sem("flag_step")
        flag_local = sem("flag_local")
        flag_step_pool = sem("flag_step_pool")
        flag_ready = sem("flag_ready")
        g_transposed = sem("g_transposed")
        g_xT = sem("g_xT")
        g_adj = sem("g_adj")
        g_xw = sem("g_xw")
        g_scores = sem("g_scores")
        g_dve = sem("g_dve")
        g_alpha = sem("g_alpha")
        g_read = sem("g_read")
        g_probs = sem("g_probs")
        g_probT = sem("g_probT")
        g_copied = sem("g_copied")
        g_mixed = sem("g_mixed")
        g_var = sem("g_var")
        g_pool = sem("g_pool")
        g_norm = sem("g_norm")
        g_stored = sem("g_stored")

        block = ctx.enter_context(nc.Block())

        def back(r, lag):
            return (r - lag) // UNITS, (r - lag) % UNITS

        def exists(tile):
            return not isinstance(tile, int) or 0 <= tile < TILES

        def first(tile, n=1):
            return isinstance(tile, int) and tile < n

        def over_pairs(eng, pair, peeled, drained=2):
            for j in range(peeled):
                pair(j)
            with eng.Fori(peeled, PAIRS) as j:
                pair(j)
            for j in range(PAIRS, PAIRS + drained):
                pair(j)

        def set_up_ps(c):
            return work_ps[:, 2 * (c % 2):2 * (c % 2) + 2, :].rearrange("p a b -> p (a b)")

        def settled(eng):
            eng.sem_inc(passed, 1)

        WARM_UP = 10
        OWN_MASKS = QUARTERS - 1
        MASK_LAG = 1
        MASKED_LAG = 2
        RELU_LAG = 3
        EXP_LAG = 10
        T_LAG = 13
        HI_LAG = T_LAG
        LO_LAG = T_LAG + 1
        MIX_LAG = T_LAG + 2
        X_HIGH_AT = (11, 13)
        X_LOW_AT = (11, 12, 14, 15)
        XWT_HIGH_AT = (1, 5, 9)
        XWT_LOW_AT = (7, 11, 15)

        @block.sync
        def _(sp):
            n = TILES // QUARTERS
            for c in range(QUARTERS):
                sp.dma_start(x[:, n * c:n * c + n, :], x_rows[:, n * c:n * c + n, :]).then_inc(x_loaded[c], 16)
                if c == 1:
                    sp.dma_start(adj[:, 0, 0:N // 2], adj_tiles[:, 0, 0:N // 2]).then_inc(adj_begun, 16)
            sp.dma_start(adj[:, 0, N // 2:N], adj_tiles[:, 0, N // 2:N]).then_inc(adj_loaded[0], 16)
            sp.dma_start(adj[:, 1, :], adj_tiles[:, 1, :]).then_inc(adj_loaded[1], 16)

            STORE_LAG = 5

            def pair(j):
                for s in range(2):
                    i = 2 * j + s
                    if exists(i) and not first(i, 2):
                        sp.wait_ge(mask_ready, OWN_MASKS * (i - 1))
                        sp.wait_ge(mask_last_ready, i - 1)
                        sp.dma_start(adj[:, s, :], adj_tiles[:, bass.ds(i, 1), :]).then_inc(adj_loaded[s], 16)
                    k = i - STORE_LAG
                    if exists(k):
                        store(k, 1 - s)

            def store(k, s):
                sp.wait_ge(norm_ready, k + 1)
                sp.dma_start(out_tiles[:, bass.ds(k, 1), :], normed[:, s, :]).then_inc(stored[s], 16)

            over_pairs(sp, pair, peeled=3, drained=3)
            for s in range(2):
                sp.wait_ge(stored[s], 16 * PAIRS)

            sp.wait_ge(flag_ready, 1)
            general = sp.value_load(flag_word[0:1, 0:1], min_val=0, max_val=1)
            with sp.If(general > 0):
                with sp.Fori(0, TILES) as t:
                    sp.dma_start(adj[:, 0, :], adj_tiles[:, bass.ds(t, 1), :]).then_inc(g_adj, 16)
                    sp.wait_ge(g_norm, t + 1)
                    sp.dma_start(out_tiles[:, bass.ds(t, 1), :], normed[:, 0, :]).then_inc(g_stored, 16)
                sp.wait_ge(g_stored, 16 * TILES)
            sp.nop()

        @block.gpsimd
        def _(pool):
            nc.gpsimd.memset(ident[:, :], 0.0).then_inc(cleared, 1)
            nc.gpsimd.memset(minus_half[:, :], -0.5).then_inc(cleared, 1)
            pool.wait_ge(cleared, 2)
            nc.gpsimd.affine_select(out=ident[:, :], in_=ident[:, :], compare_op=ALU.not_equal, fill=1.0, base=0,
                                    pattern=[[-1, P]], channel_multiplier=1).then_inc(ident_ready, 1)

            def make_mask(i, s):
                pool.wait_ge(adj_loaded[s], 8 * (i - s) + 16)
                if not first(i, 2):
                    pool.wait_ge(masked_ready, QUARTERS * i - QUARTERS)
                settled(pool)
                nc.gpsimd.tensor_scalar(mask_last[:, s, :], adj[:, s, N - HALF:N], -1.0, BIG,
                                        ALU.add, ALU.mult).then_inc(mask_last_ready, 1)

            def leaky(i, s, c):
                q = QUARTERS * i + c
                part = probs[:, s, HALF * c:HALF * c + HALF]
                pool.wait_ge(relu_ready, q + 1)
                nc.gpsimd.tensor_tensor(part, part, relu[:, c % 2, :], ALU.add).then_inc(leaky_ready, 1)

            def layer_norm(i, s):
                pool.wait_ge(var_ready, i + 1)
                settled(pool)
                nc.gpsimd.tensor_scalar(var_eps[:, s:s + 1], mean_var[:, s, 1:2], EPS, None,
                                        ALU.add).then_inc(eps_added, 1)
                pool.wait_ge(eps_added, i + 1)
                nc.gpsimd.tensor_tensor(rstd[:, s:s + 1], var_eps[:, s:s + 1], minus_half[:, :],
                                        ALU.pow).then_inc(rstd_ready, 1)
                pool.wait_ge(rstd_ready, i + 1)
                if not first(i, 2):
                    pool.wait_ge(stored[s], 8 * (i - s))
                settled(pool)
                nc.gpsimd.tensor_scalar(normed[:, s, :], y[:, s, :], mean_var[:, s, 0:1], rstd[:, s:s + 1],
                                        ALU.subtract, ALU.mult).then_inc(norm_ready, 1)

            def make_first_mask(c):
                pool.wait_ge(adj_begun, 16)
                nc.gpsimd.tensor_scalar(mask[:, c % 2, :], adj[:, 0, HALF * c:HALF * c + HALF], -1.0, BIG,
                                        ALU.add, ALU.mult).then_inc(mask_ready, 1)

            make_first_mask(0)
            make_first_mask(1)
            make_mask(0, 0)

            def pair(j):
                for s in range(2):
                    i = 2 * j + s
                    for c in range(QUARTERS):
                        if exists(i):
                            leaky(i, s, c)
                        if exists(i) and c == QUARTERS - 1:
                            nc.gpsimd.tensor_copy(row_max[:, bass.ds(i, 1)],
                                                  chunk_max[:, s, QUARTERS - 1:QUARTERS]).then_inc(max_kept, 1)
                        if c == 1 and exists(i - 3):
                            layer_norm(i - 3, 1 - s)
                        if c == 1 and exists(i + 1):
                            make_mask(i + 1, 1 - s)

            for j in range(3):
                pair(j)
            with pool.Fori(3, PAIRS - 1) as j:
                pair(j)
            for j in range(PAIRS - 1, PAIRS + 1):
                pair(j)

            pool.wait_ge(flag_local, 1)
            nc.gpsimd.partition_all_reduce(flag_max[:, :], flag_row[:, :], P,
                                           bass.bass_isa.ReduceOp.max).then_inc(flag_step_pool, 1)
            pool.wait_ge(flag_step_pool, 1)
            nc.gpsimd.tensor_scalar(flag_word[:, :], flag_max[:, :], 1.0, None, ALU.is_gt).then_inc(flag_ready, 1)
            layer_norm(TILES - 1, 1)
            pool.wait_ge(flag_ready, 1)
            general = pool.value_load(flag_word[0:1, 0:1], min_val=0, max_val=1)
            with pool.If(general > 0):
                for s in range(2):
                    pool.wait_ge(stored[s], 16 * PAIRS)
                with pool.Fori(0, TILES) as t:
                    pool.wait_ge(g_var, t + 1)
                    settled(pool)
                    nc.gpsimd.tensor_scalar(var_eps[:, 0:1], mean_var[:, 0, 1:2], EPS, None,
                                            ALU.add).then_inc(g_pool, 1)
                    pool.wait_ge(g_pool, 2 * t + 1)
                    nc.gpsimd.tensor_tensor(rstd[:, 0:1], var_eps[:, 0:1], minus_half[:, :],
                                            ALU.pow).then_inc(g_pool, 1)
                    pool.wait_ge(g_pool, 2 * t + 2)
                    settled(pool)
                    nc.gpsimd.tensor_scalar(normed[:, 0, :], y[:, 0, :], mean_var[:, 0, 0:1], rstd[:, 0:1],
                                            ALU.subtract, ALU.mult).then_inc(g_norm, 1)
                    pool.wait_ge(g_stored, 16 * t + 16)
            pool.nop()

        @block.tensor
        def _(pe):
            def make_xT(c):
                pe.wait_ge(x_loaded[c], 16)
                if c >= 2:
                    pe.wait_ge(xT_split, c - 1)
                if c == 2:
                    pe.wait_ge(xwT_split, 1)
                elif c == 3:
                    pe.wait_ge(xwT_kept, 1)
                for k in range(HALF // P):
                    last = nc.tensor.transpose(set_up_ps(c)[:, P * k:P * k + P], x[:, HALF // P * c + k, :],
                                               ident[:, :])
                last.then_inc(xT_ready, 1)

            pe.wait_ge(ident_ready, 1)
            for k in range(WARM_UP):
                nc.tensor.transpose(score_ps[:, 1, 0:P], ident[:, :], ident[:, :])
            make_xT(0)
            make_xT(1)

            def scores(j, r):
                off, u = back(r, 0)
                i = 2 * j + off
                if not exists(i):
                    return
                c, h = u // 2, u % 2
                if first(i):
                    if h == 0:
                        first_scores(c)
                    return
                if u == 0 and first(i, 2):
                    pe.wait_ge(xwT_split, 1)
                if h == 0 and not (isinstance(i, int) and QUARTERS * i + c < 2):
                    pe.wait_ge(masked_ready, QUARTERS * i + c - 1)
                out = score_ps[:, c % 2, h * BANK:h * BANK + BANK]
                cols = slice(u * BANK, u * BANK + BANK)
                rows = bass.ds(P * i, P)
                nc.tensor.matmul(out, xwT_hi[:, rows], xT_hi[:, cols], start=True, stop=False)
                nc.tensor.matmul(out, xwT_hi[:, rows], xT_lo[:, cols], start=False, stop=False)
                nc.tensor.matmul(out, xwT_lo[:, rows], xT_hi[:, cols], start=False, stop=True)\
                    .then_inc(scores_ready, 1)

            def first_scores(c):
                pe.wait_ge(xT_hi_ready, c + 1)
                if c == 0:
                    pe.wait_ge(xwT_hi_begun, 1)
                if c >= 2:
                    pe.wait_ge(masked_ready, c - 1)
                halves = [(score_ps[:, c % 2, h * BANK:h * BANK + BANK],
                           slice(HALF * c + BANK * h, HALF * c + BANK * h + BANK)) for h in range(2)]
                for out, cols in halves:
                    nc.tensor.matmul(out, xwT_hi[:, 0:P], xT_hi[:, cols], start=True, stop=False)
                if c == 0:
                    pe.wait_ge(xwT_begun, 1)
                for out, cols in halves:
                    nc.tensor.matmul(out, xwT_lo[:, 0:P], xT_hi[:, cols], start=False, stop=False)
                pe.wait_ge(xT_split, c + 1)
                for out, cols in halves:
                    nc.tensor.matmul(out, xwT_hi[:, 0:P], xT_lo[:, cols], start=False, stop=True)\
                        .then_inc(scores_ready, 1)

            def transposes(j, r):
                off, g = back(r, T_LAG)
                i = 2 * j + off
                if not exists(i):
                    return
                if g == 0 and first(i):
                    pe.wait_ge(xT_split, QUARTERS)
                    pe.wait_ge(xwT_kept, QUARTERS - 1)
                if g % 2 == 0:
                    pe.wait_ge(probs_ready, QUARTERS * i + g // 2 + 1)
                if g >= 3 or not first(i):
                    pe.wait_ge(low_ready, UNITS * i + g - (2 if g >= 3 else 4 if g == 2 else 1))
                for k in range(BLOCKS):
                    m = g * BANK + k * P
                    last = nc.tensor.transpose(trans_ps[:, g % 3, P * k:P * k + P], probs[:, off % 2, m:m + P],
                                               ident[:, :])
                last.then_inc(transposed, 1)

            def mix(j, r):
                off, g = back(r, MIX_LAG)
                i = 2 * j + off
                if not exists(i) or g == 0:
                    return
                if g == 1:
                    if not first(i):
                        pe.wait_ge(y_ready, i)
                    mix_unit(i, 0)
                mix_unit(i, g)

            def mix_unit(i, g):
                if first(i):
                    pe.wait_ge(xparts_ready, g // 2 + 1)
                pe.wait_ge(low_ready, UNITS * i + g + 1)
                for k in range(BLOCKS):
                    m = g * BLOCKS + k
                    hi = probT_hi[:, g % 4, P * k:P * k + P]
                    lo = probT_lo[:, g % 4, P * k:P * k + P]
                    nc.tensor.matmul(mixed_ps[:, 0:2 * D], hi, xparts[:, m, :], start=(m == 0), stop=False,
                                     skip_group_check=True)
                    last = nc.tensor.matmul(mixed_ps[:, 0:D], lo, xparts[:, m, 0:D], start=False,
                                            stop=(m == TILES - 1), skip_group_check=True)
                last.then_inc(mixed, 1)

            def pair(j):
                for r in range(2 * UNITS):
                    if isinstance(j, int) and j == 2 and r == 0:
                        pe.wait_ge(xwT_split, QUARTERS)
                    scores(j, r)
                    if isinstance(j, int) and j == 0 and r == 3:
                        make_xT(2)
                        make_xT(3)
                    transposes(j, r)
                    mix(j, r)

            over_pairs(pe, pair, peeled=2)

            pe.wait_ge(flag_ready, 1)
            general = pe.value_load(flag_word[0:1, 0:1], min_val=0, max_val=1)
            with pe.If(general > 0):
                for c in range(QUARTERS):
                    if c >= 2:
                        pe.wait_ge(g_xT, c - 1)
                    for k in range(HALF // P):
                        last = nc.tensor.transpose(score_ps[:, c % 2, P * k:P * k + P],
                                                   x[:, HALF // P * c + k, :], ident[:, :])
                    last.then_inc(g_transposed, 1)
                pe.wait_ge(g_xT, QUARTERS)
                with pe.Fori(0, TILES) as t:
                    pe.wait_ge(g_xw, t + 1)
                    for n in range(HEADS * UNITS):
                        u, k = n // HEADS, n % HEADS
                        if n >= 2:
                            pe.wait_ge(g_read, HEADS * UNITS * t + n - 1)
                        nc.tensor.matmul(score_ps[:, n % 2, 0:BANK], relu[:, 0, P * k:P * k + P],
                                         probs[:, 1, u * BANK:u * BANK + BANK], start=True, stop=True)\
                            .then_inc(g_scores, 1)
                    pe.wait_ge(g_probs, t + 1)
                    for g in range(UNITS):
                        for k in range(BLOCKS):
                            m = g * BANK + k * P
                            last = nc.tensor.transpose(trans_ps[:, 0, P * k:P * k + P], probs[:, 0, m:m + P],
                                                       ident[:, :])
                        last.then_inc(g_probT, 1)
                        pe.wait_ge(g_copied, UNITS * t + g + 1)
                        for k in range(BLOCKS):
                            m = g * BLOCKS + k
                            last = nc.tensor.matmul(mixed_ps[:, 0:D], relu[:, 1, P * k:P * k + P],
                                                    x[:, m, :], start=(m == 0), stop=(m == TILES - 1))
                        last.then_inc(g_mixed, 1)
            pe.nop()

        @block.scalar
        def _(act):
            act.dma_start(w_col[:, :], w_d.rearrange("k d -> d k"), allow_slow_non_contiguous=True)\
                .then_inc(w_loaded, 16)
            act.dma_start(b_all[:, :], b_d.rearrange("(a k) -> a k", a=1).broadcast_to([P, HEADS]))\
                .then_inc(b_loaded, 16)
            act.wait_ge(cleared, 2)
            nc.scalar.activation(warm[:, :], minus_half[:, :], ACT.Exp)

            def xT_high(c):
                act.wait_ge(xT_ready, c + 1)
                nc.scalar.activation(xT_hi[:, HALF * c:HALF * c + HALF], set_up_ps(c), ACT.Copy,
                                     scale=X_SCALE).then_inc(xT_hi_ready, 1)

            def keep_xwT(c):
                act.wait_ge(xT_split, c + 1)
                nc.scalar.activation(xwT_scaled[:, HALF * c:HALF * c + HALF], set_up_ps(c), ACT.Copy,
                                     scale=w_scaled[:, :]).then_inc(xwT_kept, 1)

            def xwT_high(c):
                if c == 0:
                    act.wait_ge(xwT_begun, 1)
                    nc.scalar.activation(xwT_hi[:, P:HALF], set_up_ps(0)[:, P:HALF], ACT.Copy,
                                         scale=w_scaled[:, :]).then_inc(xwT_hi_ready, 1)
                else:
                    cols = slice(HALF * c, HALF * c + HALF)
                    act.wait_ge(xwT_kept, c)
                    nc.scalar.activation(xwT_hi[:, cols], xwT_scaled[:, cols], ACT.Copy).then_inc(xwT_hi_ready, 1)

            def x_high(c):
                rows = slice(TILES // QUARTERS * c, TILES // QUARTERS * (c + 1))
                act.wait_ge(x_loaded[c], 16)
                nc.scalar.activation(xparts[:, rows, 0:D], x[:, rows, :], ACT.Copy, scale=X_SCALE)\
                    .then_inc(xparts_hi, 1)

            x_high(0)
            xT_high(0)
            act.wait_ge(bias_ready, 1)
            nc.scalar.activation(xwT_hi[:, 0:P], set_up_ps(0)[:, 0:P], ACT.Copy, scale=w_scaled[:, :])\
                .then_inc(xwT_hi_begun, 1)
            xT_high(1)
            xwT_high(0)
            keep_xwT(1)
            x_high(1)

            def do_relu(j, r):
                off, u = back(r, RELU_LAG)
                i = 2 * j + off
                if u % 2 or not exists(i):
                    return
                q = QUARTERS * i + u // 2
                c = u // 2
                if first(i) and c == 0:
                    act.wait_ge(bias_ready, 2)
                act.wait_ge(masked_ready, q + 1)
                if not (isinstance(q, int) and q < 2):
                    act.wait_ge(leaky_ready, q - 1)
                nc.scalar.activation(relu[:, c % 2, :], probs[:, off % 2, HALF * c:HALF * c + HALF], ACT.Relu,
                                     bias=relu_bias[:, :], scale=1.0 / SLOPE - 1.0).then_inc(relu_ready, 1)

            def do_exp(j, r):
                off, u = back(r, EXP_LAG)
                i = 2 * j + off
                if u % 2 or not exists(i):
                    return
                s, c = off % 2, u // 2
                if c == 0:
                    act.wait_ge(shift_ready, i + 1)
                    if not first(i, 2):
                        act.wait_ge(sum_ready, i - 1)
                act.wait_ge(leaky_ready, QUARTERS * i + c + 1)
                part = probs[:, s, HALF * c:HALF * c + HALF]
                nc.scalar.activation(part, part, ACT.Exp, bias=shift[:, s:s + 1], scale=SLOPE / SCORE_SCALE,
                                     accum_out=part_sum[:, s, c:c + 1]).then_inc(probs_ready, 1)

            def do_high(j, r):
                off, g = back(r, HI_LAG)
                i = 2 * j + off
                if not exists(i):
                    return
                act.wait_ge(transposed, UNITS * i + g + 1)
                if not (isinstance(i, int) and UNITS * i + g < 4):
                    act.wait_ge(mixed, UNITS * i + g - 3)
                nc.scalar.activation(probT_hi[:, g % 4, :], trans_ps[:, g % 3, :], ACT.Copy,
                                     scale=PROB_SCALE).then_inc(high_ready, 1)

            def pair(j):
                for r in range(2 * UNITS):
                    do_high(j, r)
                    do_relu(j, r)
                    do_exp(j, r)
                    if isinstance(j, int) and j == 0 and r in (5, 7):
                        keep_xwT(r // 2)
                    if isinstance(j, int) and j == 1 and r in XWT_HIGH_AT:
                        xwT_high(1 + XWT_HIGH_AT.index(r))
                    if isinstance(j, int) and j == 0 and r == 3:
                        xT_high(2)
                        xT_high(3)
                    if isinstance(j, int) and j == 0 and r in X_HIGH_AT:
                        x_high(2 + X_HIGH_AT.index(r))

            over_pairs(act, pair, peeled=2)

            act.wait_ge(flag_ready, 1)
            general = act.value_load(flag_word[0:1, 0:1], min_val=0, max_val=1)
            with act.If(general > 0):
                for c in range(QUARTERS):
                    act.wait_ge(g_transposed, c + 1)
                    nc.scalar.activation(probs[:, 1, HALF * c:HALF * c + HALF], score_ps[:, c % 2, :],
                                         ACT.Copy).then_inc(g_xT, 1)
                with act.Fori(0, TILES) as t:
                    act.wait_ge(g_alpha, t + 1)
                    nc.scalar.activation(probs[:, 0, :], probs[:, 0, :], ACT.Exp, bias=shift[:, 0:1],
                                         accum_out=part_sum[:, 0, 0:1]).then_inc(g_probs, 1)
                    for g in range(UNITS):
                        act.wait_ge(g_probT, UNITS * t + g + 1)
                        if g:
                            act.wait_ge(g_mixed, UNITS * t + g)
                        nc.scalar.activation(relu[:, 1, 0:BANK], trans_ps[:, 0, :], ACT.Copy).then_inc(g_copied, 1)
            act.nop()

        @block.vector
        def _(dve):
            dve.wait_ge(w_loaded, 16)
            nc.vector.tensor_scalar(w_scaled[:, :], w_col[:, 0:1], XW_SCALE, None, ALU.mult).then_inc(bias_ready, 1)
            dve.wait_ge(bias_ready, 1)

            def split_xT(c):
                cols = slice(HALF * c, HALF * c + HALF)
                dve.wait_ge(xT_hi_ready, c + 1)
                nc.vector.scalar_tensor_tensor(out=xT_lo[:, cols], in0=set_up_ps(c), scalar=X_SCALE,
                                               in1=xT_hi[:, cols], op0=ALU.mult, op1=ALU.subtract)\
                    .then_inc(xT_split, 1)

            def split_xwT(c):
                dve.wait_ge(xwT_hi_ready, c + 1)
                if c == 0:
                    nc.vector.scalar_tensor_tensor(out=xwT_lo[:, P:HALF], in0=set_up_ps(0)[:, P:HALF],
                                                   scalar=w_scaled[:, :], in1=xwT_hi[:, P:HALF],
                                                   op0=ALU.mult, op1=ALU.subtract).then_inc(xwT_split, 1)
                else:
                    cols = slice(HALF * c, HALF * c + HALF)
                    nc.vector.tensor_tensor(xwT_lo[:, cols], xwT_scaled[:, cols], xwT_hi[:, cols],
                                            ALU.subtract).then_inc(xwT_split, 1)

            dve.wait_ge(xwT_hi_begun, 1)
            split_xT(0)
            nc.vector.scalar_tensor_tensor(out=xwT_lo[:, 0:P], in0=set_up_ps(0)[:, 0:P], scalar=w_scaled[:, :],
                                           in1=xwT_hi[:, 0:P], op0=ALU.mult, op1=ALU.subtract)\
                .then_inc(xwT_begun, 1)

            split_xT(1)

            def do_x_low(c):
                rows = slice(TILES // QUARTERS * c, TILES // QUARTERS * (c + 1))
                dve.wait_ge(xparts_hi, c + 1)
                nc.vector.scalar_tensor_tensor(out=xparts[:, rows, D:2 * D], in0=x[:, rows, :], scalar=X_SCALE,
                                               in1=xparts[:, rows, 0:D], op0=ALU.mult, op1=ALU.subtract)\
                    .then_inc(xparts_ready, 1)

            def do_set_up(r):
                if r == 1:
                    dve.wait_ge(b_loaded, 16)
                    nc.vector.tensor_scalar(relu_bias[:, :], b_all[:, 0:1], (1.0 / SLOPE - 1.0) * SCORE_SCALE, None,
                                            ALU.mult).then_inc(bias_ready, 1)
                elif r == 3:
                    split_xwT(0)
                elif r == 4:
                    split_xT(2)
                    split_xT(3)

            def do_low(j, r):
                off, g = back(r, LO_LAG)
                i = 2 * j + off
                if not exists(i):
                    return
                dve.wait_ge(high_ready, UNITS * i + g + 1)
                if not (isinstance(i, int) and UNITS * i + g < 4):
                    dve.wait_ge(mixed, UNITS * i + g - 3)
                nc.vector.scalar_tensor_tensor(out=probT_lo[:, g % 4, :], in0=trans_ps[:, g % 3, :], scalar=PROB_SCALE,
                                               in1=probT_hi[:, g % 4, :], op0=ALU.mult, op1=ALU.subtract)\
                    .then_inc(low_ready, 1)

            def do_mask(j, r):
                off, u = back(r, MASK_LAG)
                i = 2 * j + off
                if u % 2 or not exists(i):
                    return
                c, s = u // 2, off % 2
                if c == OWN_MASKS or first(i) and c < 2:
                    return
                if c == 0 or first(i):
                    dve.wait_ge(adj_loaded[s], 8 * (i - s) + 16)
                dve.wait_ge(masked_ready, QUARTERS * i + (-1, -2, 1)[c])
                nc.vector.tensor_scalar(mask[:, c % 2, :], adj[:, s, HALF * c:HALF * c + HALF], -1.0, BIG,
                                        ALU.add, ALU.mult).then_inc(mask_ready, 1)

            def do_masked(j, r):
                off, u = back(r, MASKED_LAG)
                i = 2 * j + off
                if u % 2 or not exists(i):
                    return
                c, s = u // 2, off % 2
                q = QUARTERS * i + c
                if c < OWN_MASKS:
                    dve.wait_ge(mask_ready, OWN_MASKS * i + c + 1)
                else:
                    dve.wait_ge(mask_last_ready, i + 1)
                if not first(i, 2):
                    dve.wait_ge(transposed, UNITS * i - 2 * UNITS + 2 * c + 2)
                dve.wait_ge(scores_ready, 2 * q + 2)
                if c:
                    dve.wait_ge(masked_ready, q)
                elif not first(i, 2):
                    dve.wait_ge(max_kept, i - 1)
                settled(dve)
                nc.vector.tensor_tensor_reduce(
                    out=probs[:, s, HALF * c:HALF * c + HALF], in0=score_ps[:, c % 2, :],
                    in1=mask[:, c % 2, :] if c < OWN_MASKS else mask_last[:, s, :],
                    scale=1.0, scalar=chunk_max[:, s, c - 1:c] if c else -3e38, op0=ALU.add, op1=ALU.max,
                    accum_out=chunk_max[:, s, c:c + 1]).then_inc(masked_ready, 1)

            def do_max(j, r, step):
                off, u = back(r, MASKED_LAG + (6, 7, 7)[step])
                i = 2 * j + off
                if u or not exists(i):
                    return
                s = off % 2
                m = chunk_max[:, s, QUARTERS - 1:QUARTERS]
                if step == 0:
                    dve.wait_ge(masked_ready, QUARTERS * i + QUARTERS)
                    if first(i):
                        dve.wait_ge(bias_ready, 2)
                    nc.vector.tensor_scalar(max_part[:, s:s + 1], m, PAD / SCORE_SCALE, None,
                                            ALU.mult).then_inc(max_part_ready, 1)
                    nc.vector.tensor_scalar(max_relu[:, s:s + 1], m, 1.0 / SLOPE - 1.0, relu_bias[:, :],
                                            ALU.mult, ALU.add).then_inc(max_relu_ready, 1)
                    dve.wait_ge(max_part_ready, i + 1)
                    nc.vector.scalar_tensor_tensor(out=max_pad[:, s:s + 1], in0=m, scalar=-PAD / SCORE_SCALE,
                                                   in1=max_part[:, s:s + 1], op0=ALU.mult, op1=ALU.max)\
                        .then_inc(max_pad_ready, 1)
                elif step == 1:
                    dve.wait_ge(max_relu_ready, i + 1)
                    nc.vector.scalar_tensor_tensor(out=max_sum[:, s:s + 1], in0=max_relu[:, s:s + 1], scalar=0.0,
                                                   in1=m, op0=ALU.max, op1=ALU.add).then_inc(max_sum_ready, 1)
                else:
                    dve.wait_ge(max_sum_ready, i + 1)
                    dve.wait_ge(max_pad_ready, i + 1)
                    nc.vector.scalar_tensor_tensor(out=shift[:, s:s + 1], in0=max_sum[:, s:s + 1],
                                                   scalar=-SLOPE / SCORE_SCALE, in1=max_pad[:, s:s + 1],
                                                   op0=ALU.mult, op1=ALU.subtract).then_inc(shift_ready, 1)

            def do_tail(j, r, step):
                off, u = back(r, (T_LAG + 6, T_LAG + 7, MIX_LAG + 8, MIX_LAG + 8, MIX_LAG + 9, MIX_LAG + 10)[step])
                i = 2 * j + off
                if u or not exists(i):
                    return
                s = off % 2
                if step == 0:
                    dve.wait_ge(probs_ready, QUARTERS * i + QUARTERS)
                    nc.vector.tensor_scalar(scaled_sum[:, s, :], part_sum[:, s, :], X_SCALE * PROB_SCALE, TINY_SUM,
                                            ALU.mult, ALU.add, accum_out=row_sum[:, s:s + 1]).then_inc(sum_ready, 1)
                elif step == 1:
                    dve.wait_ge(sum_ready, i + 1)
                    nc.vector.reciprocal(inv_sum[:, s:s + 1], row_sum[:, s:s + 1]).then_inc(inv_ready, 1)
                elif step == 2:
                    dve.wait_ge(inv_ready, i + 1)
                    dve.wait_ge(mixed, UNITS * i + UNITS)
                    nc.vector.scalar_tensor_tensor(out=y_hi[:, s, :], in0=mixed_ps[:, 0:D],
                                                   scalar=inv_sum[:, s:s + 1],
                                                   in1=x[:, bass.ds(i, 1), :].rearrange("p a d -> p (a d)"),
                                                   op0=ALU.mult, op1=ALU.add).then_inc(y_hi_ready, 1)
                elif step == 3:
                    dve.wait_ge(y_hi_ready, i + 1)
                    if not first(i, 2):
                        dve.wait_ge(norm_ready, i - 1)
                    nc.vector.scalar_tensor_tensor(out=y[:, s, :], in0=mixed_ps[:, D:2 * D],
                                                   scalar=inv_sum[:, s:s + 1], in1=y_hi[:, s, :],
                                                   op0=ALU.mult, op1=ALU.add).then_inc(y_ready, 1)
                elif step == 4:
                    dve.wait_ge(y_ready, i + 1)
                    nc.vector.bn_stats(stats[:, s, :], y[:, s, :]).then_inc(stats_ready, 1)
                else:
                    dve.wait_ge(stats_ready, i + 1)
                    settled(dve)
                    nc.vector.bn_aggr(mean_var[:, s, :], stats[:, s, :]).then_inc(var_ready, 1)

            def do_range_flag(j, n):
                share = N // PAIRS
                part = (xT_hi, xwT_hi)[n][:, bass.ds(share * j, share)]
                nc.vector.tensor_reduce(flag_parts[:, bass.ds(2 * j + n, 1)], part, AX.X, ALU.max,
                                        apply_absolute_value=True).then_inc(flag_step, 1)

            def do_flags():
                n = 2 * PAIRS
                dve.wait_ge(max_kept, TILES)
                nc.vector.tensor_reduce(flag_parts[:, n:n + 1], row_max[:, :], AX.X, ALU.max,
                                        apply_absolute_value=True).then_inc(flag_step, 1)
                dve.wait_ge(flag_step, n + 1)
                nc.vector.tensor_scalar(flag_scaled[:, 0:n], flag_parts[:, 0:n], 1.0 / FLAG_PART, None,
                                        ALU.mult).then_inc(flag_step, 1)
                nc.vector.tensor_scalar(flag_scaled[:, n:n + 1], flag_parts[:, n:n + 1], 1.0 / FLAG_SCORE, None,
                                        ALU.mult).then_inc(flag_step, 1)
                dve.wait_ge(flag_step, n + 3)
                nc.vector.tensor_reduce(flag_row[:, :], flag_scaled[:, :], AX.X, ALU.max).then_inc(flag_local, 1)

            def pair(j):
                for r in range(2 * UNITS):
                    do_tail(j, r, 2)
                    do_low(j, r)
                    do_tail(j, r, 3)
                    do_tail(j, r, 4)
                    do_tail(j, r, 5)
                    do_max(j, r, 1)
                    do_mask(j, r)
                    do_masked(j, r)
                    do_max(j, r, 2)
                    do_tail(j, r, 0)
                    do_tail(j, r, 1)
                    if isinstance(j, int) and j == 0:
                        do_set_up(r)
                    if isinstance(j, int) and j == 0 and r in X_LOW_AT:
                        do_x_low(X_LOW_AT.index(r))
                    if isinstance(j, int) and j == 1 and r in XWT_LOW_AT:
                        split_xwT(1 + XWT_LOW_AT.index(r))
                    if not (isinstance(j, int) and j >= PAIRS) and r in (13, 15):
                        do_range_flag(j, (r - 13) // 2)
                    if isinstance(j, int) and j == PAIRS and r == 9:
                        do_flags()
                    do_max(j, r, 0)

            over_pairs(dve, pair, peeled=2)

            dve.wait_ge(flag_ready, 1)
            general = dve.value_load(flag_word[0:1, 0:1], min_val=0, max_val=1)
            with dve.If(general > 0):
                dve.wait_ge(norm_ready, TILES)
                STEPS = HEADS + UNITS * (3 + 3 * HEADS) + 4
                with dve.Fori(0, TILES) as t:
                    done = 0

                    def own(instruction):
                        nonlocal done
                        done += 1
                        instruction.then_inc(g_dve, 1)
                        dve.wait_ge(g_dve, STEPS * t + done)

                    dve.wait_ge(g_xT, QUARTERS)
                    dve.wait_ge(g_adj, 16 * t + 16)
                    for k in range(HEADS):
                        own(nc.vector.tensor_scalar(relu[:, 0, P * k:P * k + P],
                                                    probs[:, 1, bass.ds(P * t, P)],
                                                    w_col[:, k:k + 1], None, ALU.mult))
                    nc.vector.tensor_copy(row_sum[:, 1:2], row_sum[:, 0:1]).then_inc(g_xw, 1)
                    for u in range(UNITS):
                        cols = slice(u * BANK, u * BANK + BANK)
                        alpha, a = probs[:, 0, cols], adj[:, 0, cols]
                        tmp = [adj[:, 1, n * BANK:n * BANK + BANK].bitcast(f32) for n in range(3)]
                        own(nc.vector.tensor_scalar(tmp[0], a, 1.0, NEG, ALU.is_lt, ALU.mult))
                        own(nc.vector.tensor_scalar(tmp[1], a, float(HEADS), NEG, ALU.is_gt, ALU.mult))
                        own(nc.vector.tensor_tensor(alpha, tmp[0], tmp[1], ALU.add))
                        for k in range(HEADS):
                            n = HEADS * u + k
                            dve.wait_ge(g_scores, HEADS * UNITS * t + n + 1)
                            nc.vector.tensor_scalar(tmp[0], score_ps[:, n % 2, 0:BANK], b_all[:, k:k + 1], None,
                                                    ALU.add).then_inc(g_read, 1)
                            dve.wait_ge(g_read, HEADS * UNITS * t + n + 1)
                            own(nc.vector.scalar_tensor_tensor(out=tmp[1], in0=tmp[0], scalar=SLOPE, in1=tmp[0],
                                                               op0=ALU.mult, op1=ALU.max))
                            own(nc.vector.scalar_tensor_tensor(out=tmp[2], in0=a, scalar=float(k + 1), in1=tmp[1],
                                                               op0=ALU.is_equal, op1=ALU.mult))
                            own(nc.vector.tensor_tensor(alpha, alpha, tmp[2], ALU.add))
                    own(nc.vector.tensor_reduce(chunk_max[:, 0, 0:1], probs[:, 0, :], AX.X, ALU.max))
                    nc.vector.tensor_scalar(shift[:, 0:1], chunk_max[:, 0, 0:1], -1.0, None,
                                            ALU.mult).then_inc(g_alpha, 1)
                    dve.wait_ge(g_probs, t + 1)
                    own(nc.vector.reciprocal(inv_sum[:, 0:1], part_sum[:, 0, 0:1]))
                    dve.wait_ge(g_mixed, UNITS * t + UNITS)
                    own(nc.vector.scalar_tensor_tensor(out=y[:, 0, :], in0=mixed_ps[:, 0:D],
                                                       scalar=inv_sum[:, 0:1],
                                                       in1=x[:, bass.ds(t, 1), :].rearrange("p a d -> p (a d)"),
                                                       op0=ALU.mult, op1=ALU.add))
                    own(nc.vector.bn_stats(stats[:, 0, :], y[:, 0, :]))
                    settled(dve)
                    nc.vector.bn_aggr(mean_var[:, 0, :], stats[:, 0, :]).then_inc(g_var, 1)
                    dve.wait_ge(g_norm, t + 1)
                    STEPS_USED = done
                assert STEPS_USED == HEADS + UNITS * (3 + 3 * HEADS) + 4, STEPS_USED
            dve.nop()


_INS = ["x", "adj", "L0_gnn_W", "L0_gnn_b"]


def kernel(**inputs):
    import numpy as np
    import concourse.bacc as bacc
    from concourse import mybir as mb
    from concourse.bass_utils import run_bass_kernel_spmd

    nc = bacc.Bacc("TRN2", target_bir_lowering=False, num_devices=1)
    arrays, args = {}, []
    for name in _INS:
        a = np.ascontiguousarray(inputs[name])
        arrays[f"in_{name}"] = a
        args.append(nc.dram_tensor(f"in_{name}", a.shape, mb.dt.from_np(a.dtype), kind="ExternalInput").ap())
    out = nc.dram_tensor("out", inputs["x"].shape, mb.dt.float32, kind="ExternalOutput").ap()
    graph_attention(nc, *args, out)
    return run_bass_kernel_spmd(nc, [arrays], core_ids=[0]).results[0]["out"]
```
